# Optimizing a Trainium2 kernel written in Bass

```python
import numpy as np
import jax
import jax.numpy as jnp

def _softmax(x, axis=-1):
    return jax.nn.softmax(x, axis=axis)

def _gelu(x):
    return jax.nn.gelu(x, approximate=True)

def _silu(x):
    return jax.nn.silu(x)

def _sigmoid(x):
    return jax.nn.sigmoid(x)

def _layernorm(x, axis=-1, eps=1e-05):
    m = jnp.mean(x, axis=axis, keepdims=True)
    v = jnp.var(x, axis=axis, keepdims=True)
    return (x - m) / jnp.sqrt(v + eps)

def _scatter_add(tgt, idx, src, axis=0):
    return tgt.at[idx].add(src)

def _segment_sum(src, seg, n):
    return jax.ops.segment_sum(src, seg, n)
kernel_name = 'mk_macaron_d1_jaxref_r8_098fc4'

def setup_inputs(seed: int=0):
    np.random.seed(seed)
    _w = jnp.asarray

    def _L0_attn_setup():
        import jax, jax.numpy as jnp
        import numpy as np
        B, T, D = (8, 96, 128)
        H = 16
        DH = D // H
        ROPE_BASE = 10000.0

        def _rope_tables(length, dim, dtype):
            inv_freq = 1.0 / ROPE_BASE ** (jnp.arange(0, dim, 2, dtype=jnp.float32) / dim)
            ang = jnp.arange(length, dtype=jnp.float32)[:, None] * inv_freq[None, :]
            cos = jnp.concatenate([jnp.cos(ang), jnp.cos(ang)], axis=-1).astype(dtype)
            sin = jnp.concatenate([jnp.sin(ang), jnp.sin(ang)], axis=-1).astype(dtype)
            return (cos, sin)

        def _rotate_half(x):
            half = x.shape[-1] // 2
            return jnp.concatenate([-x[..., half:], x[..., :half]], axis=-1)

        def _apply_rope(x, cos, sin):
            return x * cos[None, None] + _rotate_half(x) * sin[None, None]
        key = jax.random.key(seed)
        kx, kw, kb = jax.random.split(key, 3)
        x = jax.random.normal(kx, (B, T, D), dtype=jnp.float32)
        bound = 1.0 / np.sqrt(D)
        W_qkv = jax.random.uniform(kw, (3 * D, D), dtype=jnp.float32, minval=-bound, maxval=bound)
        b_qkv = jax.random.uniform(kb, (3 * D,), dtype=jnp.float32, minval=-bound, maxval=bound)
        return {'x': x, 'W_qkv': W_qkv, 'b_qkv': b_qkv}
    _L0_attn_in = _L0_attn_setup()

    def _L0_ffn_setup():
        import jax, jax.numpy as jnp
        import numpy as np
        B, S, D = (2, 256, 128)
        E, G, K = (32, 8, 4)
        H, SH = (256, 256)
        CAP_FACTOR = 1.25

        def _l2norm(v):
            n = jnp.linalg.norm(v, axis=-1, keepdims=True)
            return v / jnp.maximum(n, 1e-12)
        key = jax.random.key(seed)
        ks = jax.random.split(key, 10)
        x = jax.random.normal(ks[0], (B, S, D), jnp.float32)
        group_centroids = jax.random.normal(ks[1], (G, D), jnp.float32) * 0.02
        expert_centroids = jax.random.normal(ks[2], (E, D), jnp.float32) * 0.02
        bias = jnp.zeros((E,), jnp.float32)
        sd_in = 1.0 / np.sqrt(D).astype(np.float32)
        sd_h = 1.0 / np.sqrt(H).astype(np.float32)
        wg = jax.random.normal(ks[3], (E, D, H), jnp.float32) * sd_in
        wu = jax.random.normal(ks[4], (E, D, H), jnp.float32) * sd_in
        wd = jax.random.normal(ks[5], (E, H, D), jnp.float32) * sd_h
        sg = jax.random.normal(ks[6], (D, SH), jnp.float32) * sd_in
        su = jax.random.normal(ks[7], (D, SH), jnp.float32) * sd_in
        sd_w = jax.random.normal(ks[8], (SH, D), jnp.float32) * sd_h
        return dict(x=x, group_centroids=group_centroids, expert_centroids=expert_centroids, bias=bias, wg=wg, wu=wu, wd=wd, sg=sg, su=su, sd=sd_w)
    _L0_ffn_in = _L0_ffn_setup()
    _d = {'L0_attn_x': _L0_attn_in['x'], 'L0_attn_W_qkv': _L0_attn_in['W_qkv'], 'L0_attn_b_qkv': _L0_attn_in['b_qkv'], 'L0_ffn_group_centroids': _L0_ffn_in['group_centroids'], 'L0_ffn_expert_centroids': _L0_ffn_in['expert_centroids'], 'L0_ffn_bias': _L0_ffn_in['bias'], 'L0_ffn_wg': _L0_ffn_in['wg'], 'L0_ffn_wu': _L0_ffn_in['wu'], 'L0_ffn_wd': _L0_ffn_in['wd'], 'L0_ffn_sg': _L0_ffn_in['sg'], 'L0_ffn_su': _L0_ffn_in['su'], 'L0_ffn_sd': _L0_ffn_in['sd']}
    _x0 = _d['L0_attn_x']
    _d['L0_attn_x'] = jax.random.normal(jax.random.fold_in(jax.random.key(seed), 1), (1, 2048, 128), dtype=_x0.dtype)
    del _x0
    return _d

def reference(L0_attn_x, L0_attn_W_qkv, L0_attn_b_qkv, L0_ffn_group_centroids, L0_ffn_expert_centroids, L0_ffn_bias, L0_ffn_wg, L0_ffn_wu, L0_ffn_wd, L0_ffn_sg, L0_ffn_su, L0_ffn_sd):

    def _L0_attn_ref(x, W_qkv, b_qkv):
        import jax, jax.numpy as jnp
        import numpy as np
        B, T, D = (8, 96, 128)
        H = 16
        DH = D // H
        ROPE_BASE = 10000.0

        def _rope_tables(length, dim, dtype):
            inv_freq = 1.0 / ROPE_BASE ** (jnp.arange(0, dim, 2, dtype=jnp.float32) / dim)
            ang = jnp.arange(length, dtype=jnp.float32)[:, None] * inv_freq[None, :]
            cos = jnp.concatenate([jnp.cos(ang), jnp.cos(ang)], axis=-1).astype(dtype)
            sin = jnp.concatenate([jnp.sin(ang), jnp.sin(ang)], axis=-1).astype(dtype)
            return (cos, sin)

        def _rotate_half(x):
            half = x.shape[-1] // 2
            return jnp.concatenate([-x[..., half:], x[..., :half]], axis=-1)

        def _apply_rope(x, cos, sin):
            return x * cos[None, None] + _rotate_half(x) * sin[None, None]
        batch, length, dim = x.shape
        qkv = x @ W_qkv.T + b_qkv
        q, k, v = jnp.split(qkv, 3, axis=-1)

        def to_heads(t):
            return t.reshape(batch, length, H, DH).transpose(0, 2, 1, 3)
        q, k, v = (to_heads(q), to_heads(k), to_heads(v))
        cos, sin = _rope_tables(length, DH, x.dtype)
        q = _apply_rope(q, cos, sin)
        k = _apply_rope(k, cos, sin)
        scores = jnp.einsum('bhtd,bhsd->bhts', q, k)
        mask = jnp.tril(jnp.ones((length, length), dtype=x.dtype))
        retention = scores * mask[None, None]
        out = jnp.einsum('bhts,bhsd->bhtd', retention, v)
        return out.transpose(0, 2, 1, 3).reshape(batch, length, dim)

    def _L0_ffn_ref(x, group_centroids, expert_centroids, bias, wg, wu, wd, sg, su, sd):
        import jax, jax.numpy as jnp
        import numpy as np
        B, S, D = (2, 256, 128)
        E, G, K = (32, 8, 4)
        H, SH = (256, 256)
        CAP_FACTOR = 1.25

        def _l2norm(v):
            n = jnp.linalg.norm(v, axis=-1, keepdims=True)
            return v / jnp.maximum(n, 1e-12)
        b, s, d = x.shape
        xf = x.reshape(-1, d)
        N = xf.shape[0]
        shared = jax.nn.silu(xf @ sg) * (xf @ su) @ sd
        xn = _l2norm(xf)
        group_scores = xn @ _l2norm(group_centroids).T
        n_top_groups = max(1, G // 2)
        _, top_group_idx = jax.lax.top_k(group_scores, n_top_groups)
        expert_scores = xn @ _l2norm(expert_centroids).T + bias
        expert_to_group = jnp.arange(E) // (E // G)
        sel = jnp.zeros((N, G), xf.dtype).at[jnp.arange(N)[:, None], top_group_idx].set(1.0)
        group_mask = sel[:, expert_to_group]
        masked = expert_scores * group_mask + (1.0 - group_mask) * -1000000000.0
        top_scores, top_idx = jax.lax.top_k(masked, K)
        gates = jax.nn.softmax(top_scores, axis=-1)
        capacity = max(1, int(N / E * K * CAP_FACTOR))
        flat_e = top_idx.reshape(-1)
        flat_g = gates.reshape(-1)
        tok = jnp.repeat(jnp.arange(N), K)
        onehot = jax.nn.one_hot(flat_e, E, dtype=jnp.int32)
        pos = jnp.cumsum(onehot, axis=0)[jnp.arange(N * K), flat_e] - 1
        keep = pos < capacity
        e_s = jnp.where(keep, flat_e, E)
        p_s = jnp.where(keep, pos, 0)
        buf = jnp.zeros((E + 1, capacity, d), xf.dtype).at[e_s, p_s].set(xf[tok])[:E]
        h = jax.nn.silu(jnp.einsum('ecd,edh->ech', buf, wg)) * jnp.einsum('ecd,edh->ech', buf, wu)
        out_e = jnp.einsum('ech,ehd->ecd', h, wd)
        gathered = out_e[flat_e, jnp.minimum(pos, capacity - 1)]
        contrib = gathered * (flat_g * keep.astype(xf.dtype))[:, None]
        routed = jnp.zeros_like(xf).at[tok].add(contrib)
        return (shared + routed).reshape(b, s, d)
    x = L0_attn_x
    x = x + 0.5 * _L0_ffn_ref(_layernorm(x, axis=-1), L0_ffn_group_centroids, L0_ffn_expert_centroids, L0_ffn_bias, L0_ffn_wg, L0_ffn_wu, L0_ffn_wd, L0_ffn_sg, L0_ffn_su, L0_ffn_sd)
    x = x + _L0_attn_ref(_layernorm(x, axis=-1), L0_attn_W_qkv, L0_attn_b_qkv)
    x = x + 0.5 * _L0_ffn_ref(_layernorm(x, axis=-1), L0_ffn_group_centroids, L0_ffn_expert_centroids, L0_ffn_bias, L0_ffn_wg, L0_ffn_wu, L0_ffn_wd, L0_ffn_sg, L0_ffn_su, L0_ffn_sd)
    return x

_drawn_inputs = setup_inputs


def setup_inputs(seed=0):
    import zlib

    import numpy as np

    out = dict(_drawn_inputs(seed))
    spreads = {'L0_ffn_bias': (0.0, 0.1)}
    factors = {}
    for name, (base, spread) in spreads.items():
        noise = np.random.default_rng([zlib.crc32(name.encode()), seed]).standard_normal(out[name].shape)
        drawn = base * np.exp(spread * noise) if base else spread * noise
        out[name] = jnp.asarray(drawn.astype(out[name].dtype))
    for name, factor in factors.items():
        out[name] = (out[name] * factor).astype(out[name].dtype)
    return out
```

```python
from contextlib import ExitStack

import numpy as np

import concourse.bass as bass
from concourse import mybir

F32 = mybir.dt.float32
U32 = mybir.dt.uint32
ALU = mybir.AluOpType
ACT = mybir.ActivationFunctionType
AX = mybir.AxisListType

P = 128
D = 128
TOKENS = 2048
TILES = TOKENS // P
GT = 4
GROUPS = TILES // GT
GW = GT * P
E = 32
NG = 8
EPG = E // NG
K = 4
H = 256
HC = H // P
CAP = max(1, int(TOKENS / E * K * 1.25))
FULL = CAP // P
REST = CAP - FULL * P
ST = FULL + 1
SLOTS = E * CAP
FAR = 1 << 16
ROW = D + 2
HEADS = 16
DH = D // HEADS
HB = 4
ROPE_BASE = 10000.0
LN_EPS = 1e-5
SIZES = [P] * FULL + [REST]
XB = 4

C_IDENT, C_TRI, C_STRICT, C_ONES, C_BLOCK = (i * P for i in range(5))
C_HEAD = 5 * P
C_IOTA = C_HEAD + HB
C_COS = C_IOTA + E
C_SIN = C_COS + TILES * DH
C_ALL = C_SIN + TILES * DH


def shape_constants():
    c = np.zeros((P, C_ALL), np.float32)
    i = np.arange(P)
    c[:, C_IDENT:C_IDENT + P] = i[:, None] == i[None, :]
    c[:, C_TRI:C_TRI + P] = i[:, None] <= i[None, :]
    c[:, C_STRICT:C_STRICT + P] = i[:, None] < i[None, :]
    c[:, C_ONES:C_ONES + P] = 1.0
    c[:, C_BLOCK:C_BLOCK + P] = i[:, None] // DH == i[None, :] // DH
    c[:, C_HEAD:C_HEAD + HB] = (i[:, None] // DH) % HB == np.arange(HB)[None, :]
    c[:, C_IOTA:C_IOTA + E] = np.arange(E)[None, :]
    freq = np.float32(1) / np.float32(ROPE_BASE) ** (np.arange(0, DH, 2, dtype=np.float32) / np.float32(DH))
    ang = np.arange(TOKENS, dtype=np.float32)[:, None] * freq[None, :]
    cos = np.concatenate([np.cos(ang), np.cos(ang)], 1)
    sin = np.concatenate([-np.sin(ang), np.sin(ang)], 1)
    for at, t in ((C_COS, cos), (C_SIN, sin)):
        c[:, at:at + TILES * DH] = t.reshape(TILES, P, DH).transpose(1, 0, 2).reshape(P, -1)
    place = (np.arange(TILES)[None, :, None] * P + i[:, None, None]) * K + np.arange(K)[None, None, :]
    return c, np.ascontiguousarray(place.reshape(P, TILES * K)).astype(np.uint32)


def macaron(nc, x, consts, places, wqkv, bqkv, cents, ebias, ew, sgu, sd, out):
    x_t = x.rearrange("(t p) d -> p t d", p=P)
    out_t = out.rearrange("(t p) d -> p t d", p=P)

    with ExitStack() as ctx:
        def sb(name, shape, dt=F32):
            return ctx.enter_context(nc.sbuf_tensor(name, shape, dt))

        def sem(name):
            return ctx.enter_context(nc.semaphore(name))

        slots = [nc.dram_tensor(f"slots{f}", [SLOTS, ROW], F32, kind="Internal").ap() for f in range(2)]
        routed = [nc.dram_tensor(f"routed{f}", [TOKENS * K, D], F32, kind="Internal").ap() for f in range(2)]

        bank = [ctx.enter_context(nc.psum_tensor(f"bank{i}", [P, 512], F32)) for i in range(8)]

        cst = sb("cst", [P, C_ALL])
        plc = sb("plc", [P, TILES * K], U32)
        w_qkv = sb("w_qkv", [P, 3 * D])
        b_qkv = sb("b_qkv", [P, 3 * D])
        cen = sb("cen", [NG + E, D])
        cen_sq = sb("cen_sq", [NG + E, D])
        cen_n = sb("cen_n", [NG + E, 4])
        cenT = sb("cenT", [P, NG + E])
        e_bias = sb("e_bias", [P, E])
        w_sgu = sb("w_sgu", [P, 2 * H])
        w_sd = sb("w_sd", [P, HC * D])
        zeros = sb("zeros", [P, 2048])
        empty = sb("empty", [P, 10 * ROW])

        xres = sb("xres", [P, TILES * D])
        st = sb("st", [P, GT, 6])
        mv = sb("mv", [P, GT, 2])
        ve = sb("ve", [P, GT])
        sq = sb("sq", [P, 2, GT])
        rs = sb("rs", [P, 2, GT])
        rn0 = sb("rn0", [P, GT])
        rn = sb("rn", [P, GT])
        xf = sb("xf", [P, GT, D])
        xfT = sb("xfT", [P, GW])

        gs = sb("gs", [P, HC, GW])
        hs = sb("hs", [P, HC, GW])
        sc = sb("sc", [P, GT, NG + E])
        es = sb("es", [P, GT, E])
        g8 = sb("g8", [P, GT, 8])
        gi8 = sb("gi8", [P, GT, 8], U32)
        gif = sb("gif", [P, GT, K])
        geq = sb("geq", [P, GT * K, NG])
        gm = sb("gm", [P, GT, NG])
        pen = sb("pen", [P, GT, NG])
        mk0 = sb("mk0", [P, GT * NG, EPG])
        mk = sb("mk", [P, GT * NG, EPG])
        v8 = sb("v8", [P, GT, 8])
        vi8 = sb("vi8", [P, GT, 8], U32)
        eif = sb("eif", [P, GT, K])
        dlt = sb("dlt", [P, GT, K])
        th = sb("th", [P, GT, K])
        num = sb("num", [P, GT, K])
        den = sb("den", [P, GT, K])
        rden = sb("rden", [P, GT, K])
        ex = sb("ex", [P, GT, K])
        sm = sb("sm", [P, GT])
        rsm = sb("rsm", [P, GT])
        oh = sb("oh", [P, GT * K, E])
        cnt = sb("cnt", [P, GT, E])
        seen = sb("seen", [P, GT + 1, E])
        pe_ = sb("pe_", [P, GT * K, E])
        pos = sb("pos", [P, GT * K])
        far = sb("far", [P, GT * K])
        slot0 = sb("slot0", [P, GT * K])
        slot = sb("slot", [P, GT * K], U32)
        rows = sb("rows", [P, GT, K, ROW])

        w_e = [sb(f"w_e{b}", [P, 3 * H]) for b in range(2)]
        xb = [sb(f"xb{b}", [P, ST, ROW]) for b in range(XB)]
        xbT = [sb(f"xbT{b}", [P, CAP]) for b in range(2)]
        eg = sb("eg", [P, HC, CAP])
        eh = [sb(f"eh{b}", [P, HC, CAP]) for b in range(2)]
        eo = [sb(f"eo{b}", [P, ST, D]) for b in range(2)]

        yk = sb("yk", [P, GT, K * D])
        y2 = sb("y2", [P, GT, 2 * D])
        y1 = sb("y1", [P, GT, D])

        qkv = [sb(f"qkv{b}", [P, 3 * D]) for b in range(2)]
        rc = sb("rc", [P, 2 * HEADS, DH])
        rr = sb("rr", [P, 2 * HEADS, DH])
        qk = [sb(f"qk{b}", [P, 2 * D]) for b in range(2)]
        qkT = [sb(f"qkT{b}", [P, 2 * P]) for b in range(2)]
        qx = sb("qx", [P, HB, P])
        pr = sb("pr", [P, HB, 4 * P])
        kvm = sb("kvm", [P, D])
        state = sb("state", [P, D])

        ident = cst[:, C_IDENT:C_IDENT + P]
        tri = cst[:, C_TRI:C_TRI + P]
        strict = cst[:, C_STRICT:C_STRICT + P]
        ones = cst[:, C_ONES:C_ONES + P]
        block_mask = cst[:, C_BLOCK:C_BLOCK + P]
        head_mask = cst[:, C_HEAD:C_HEAD + HB]
        iota = cst[:, C_IOTA:C_IOTA + E]

        names = """consts_in small_in x_in empty_set empty_sent0 zeros_sent0 slots_sent routed_sent
            empty_sent1 zeros_sent1 cen_in cen_square cen_root cen_inv0 cen_inv cen_scaled cen_turned cenT_ready
            stats mean_var var_eps var_inv sq_ready roots xf_ready xf_turned xfT_ready
            norm_floor norm_inv router_out gates_up shared_gate shared_hidden shared_out base_ready
            scores_n es_ready g_top g_idx g_idxf g_eq g_mask g_pen mk_half mk_ready v_top v_idx v_idxf
            delta tanh_ready e_num e_den e_rden e_exp e_sum e_rsum hot count seen_ready prefix_out
            rows_free results_free pos_part pos_ready far_ready slot_half slot_ready rows_x rows_gate
            x_turned xT_ready e_gate_out e_up_out e_gate_act e_hidden e_down e_scaled
            yk_in y_pairs y_sum x1_ready qkv_out qkv_biased rope_parts rope_ready qk_turned qkT_ready
            qx_ready score_out masked attn_out kv_out x2_ready kv_masked state_ready out_sent""".split()
        S = {n: sem(n) for n in names}
        passed = {e: sem(f"passed_{e}") for e in ("dve", "pool")}
        AHEAD = 1
        s_w = [sem(f"weights_in{b}") for b in range(2)]
        s_xb = [sem(f"slots_in{b}") for b in range(XB)]
        s_sc = [sem(f"results_sent{b}") for b in range(XB)]

        block = ctx.enter_context(nc.Block())

        def bc(ap, axis, n):
            shape = list(ap.shape)
            shape.insert(axis, n)
            return ap.unsqueeze(axis).to_broadcast(shape)

        def expert(f, i, d):
            return XB * i + (E * f + d)

        def sent_count(f, i, d):
            return (i + (E // XB * f + d // XB + 1)) * (16 * ST)

        def xres_of(g):
            return xres[:, bass.ds(g * GW, GW)].rearrange("p (j d) -> p j d", j=GT)

        def ln_pass(f, g, second=True):
            return g if f == 0 else GROUPS + 2 * g + (1 if second else 0)

        @block.vector
        def _(dve):
            def norm(n, g):
                xr = xres_of(g)
                for j in range(GT):
                    i = nc.vector.bn_stats(st[:, j, :], xr[:, j, :])
                i.then_inc(S["stats"], 1)
                dve.wait_ge(S["stats"], n + 1)
                dve.sem_inc(passed["dve"], 1)
                for j in range(GT):
                    i = nc.vector.bn_aggr(mv[:, j, :], st[:, j, :])
                i.then_inc(S["mean_var"], 1)
                dve.wait_ge(S["mean_var"], n + 1)
                nc.vector.tensor_scalar(ve[:], mv[:, :, 1], LN_EPS, None, ALU.add).then_inc(S["var_eps"], 1)
                dve.wait_ge(S["var_eps"], n + 1)
                nc.vector.reciprocal(sq[:, 0, :], ve[:]).then_inc(S["var_inv"], 1)
                dve.wait_ge(S["var_inv"], n + 1)
                nc.vector.scalar_tensor_tensor(out=sq[:, 1, :], in0=mv[:, :, 1], scalar=float(D), in1=sq[:, 0, :],
                                               op0=ALU.mult, op1=ALU.mult).then_inc(S["sq_ready"], 1)
                dve.wait_ge(S["roots"], n + 1)
                for j in range(GT):
                    nc.vector.tensor_scalar(xf[:, j, :], xr[:, j, :], mv[:, j, 0:1], rs[:, 0, j:j + 1],
                                            ALU.subtract, ALU.mult).then_inc(S["xf_ready"], 1)

            def route(q, n, g):
                nc.vector.tensor_scalar(rn0[:], rs[:, 1, :], 1e-12, None, ALU.max).then_inc(S["norm_floor"], 1)
                dve.wait_ge(S["norm_floor"], q + 1)
                nc.vector.reciprocal(rn[:], rn0[:]).then_inc(S["norm_inv"], 1)
                dve.wait_ge(S["norm_inv"], q + 1)
                dve.wait_ge(S["router_out"], q + 1)
                nc.vector.tensor_tensor(sc[:], bank[1][:, 0:GT * (NG + E)].rearrange("p (j e) -> p j e", j=GT),
                                        bc(rn[:], 2, NG + E), ALU.mult).then_inc(S["scores_n"], 1)
                dve.wait_ge(S["scores_n"], q + 1)
                nc.vector.tensor_tensor(es[:], sc[:, :, NG:], bc(e_bias[:], 1, GT), ALU.add).then_inc(S["es_ready"], 1)
                for j in range(GT):
                    i = nc.vector.max(g8[:, j, :], sc[:, j, 0:NG])
                i.then_inc(S["g_top"], 1)
                dve.wait_ge(S["g_top"], q + 1)
                dve.sem_inc(passed["dve"], 1)
                for j in range(GT):
                    i = nc.vector.max_index(gi8[:, j, :], g8[:, j, :], sc[:, j, 0:NG])
                i.then_inc(S["g_idx"], 1)
                dve.wait_ge(S["g_idx"], q + 1)
                nc.vector.tensor_copy(gif[:], gi8[:, :, 0:K]).then_inc(S["g_idxf"], 1)
                dve.wait_ge(S["g_idxf"], q + 1)
                nc.vector.tensor_tensor(geq[:], bc(gif[:].rearrange("p j k -> p (j k)"), 2, NG),
                                        bc(iota[:, 0:NG], 1, GT * K), ALU.is_equal).then_inc(S["g_eq"], 1)
                dve.wait_ge(S["g_eq"], q + 1)
                nc.vector.tensor_reduce(gm[:], geq[:].rearrange("p (j k) g -> p j g k", k=K), AX.X,
                                        ALU.add).then_inc(S["g_mask"], 1)
                dve.wait_ge(S["g_mask"], q + 1)
                nc.vector.tensor_scalar(pen[:], gm[:], 1e9, -1e9, ALU.mult, ALU.add).then_inc(S["g_pen"], 1)
                dve.wait_ge(S["es_ready"], q + 1)
                nc.vector.tensor_tensor(mk0[:], es[:].rearrange("p j (g e) -> p (j g) e", e=EPG),
                                        bc(gm[:].rearrange("p j g -> p (j g)"), 2, EPG), ALU.mult).then_inc(S["mk_half"], 1)
                dve.wait_ge(S["mk_half"], q + 1)
                dve.wait_ge(S["g_pen"], q + 1)
                nc.vector.tensor_tensor(mk[:], mk0[:], bc(pen[:].rearrange("p j g -> p (j g)"), 2, EPG),
                                        ALU.add).then_inc(S["mk_ready"], 1)
                dve.wait_ge(S["mk_ready"], q + 1)
                dve.sem_inc(passed["dve"], 1)
                mkj = mk[:].rearrange("p (j g) e -> p j (g e)", j=GT)
                for j in range(GT):
                    i = nc.vector.max(v8[:, j, :], mkj[:, j, :])
                i.then_inc(S["v_top"], 1)
                dve.wait_ge(S["v_top"], q + 1)
                dve.sem_inc(passed["dve"], 1)
                for j in range(GT):
                    i = nc.vector.max_index(vi8[:, j, :], v8[:, j, :], mkj[:, j, :])
                i.then_inc(S["v_idx"], 1)
                nc.vector.tensor_tensor(dlt[:], v8[:, :, 0:K], v8[:, :, 0:1].to_broadcast([P, GT, K]),
                                        ALU.subtract).then_inc(S["delta"], 1)
                dve.wait_ge(S["v_idx"], q + 1)
                nc.vector.tensor_copy(eif[:], vi8[:, :, 0:K]).then_inc(S["v_idxf"], 1)
                dve.wait_ge(S["v_idxf"], q + 1)
                nc.vector.tensor_tensor(oh[:], bc(eif[:].rearrange("p j k -> p (j k)"), 2, E),
                                        bc(iota, 1, GT * K), ALU.is_equal).then_inc(S["hot"], 1)
                dve.wait_ge(S["hot"], q + 1)
                nc.vector.tensor_reduce(cnt[:], oh[:].rearrange("p (j k) e -> p j e k", k=K), AX.X,
                                        ALU.add).then_inc(S["count"], 1)
                dve.wait_ge(S["count"], q + 1)
                dve.wait_ge(S["seen_ready"], (GT + 1) * q + AHEAD)
                for j in range(GT):
                    nc.vector.tensor_tensor(seen[:, j + 1, :], seen[:, j, :], cnt[:, j, :],
                                            ALU.add).then_inc(S["seen_ready"], 1)
                    dve.wait_ge(S["seen_ready"], (GT + 1) * q + j + 1 + AHEAD)
                dve.wait_ge(S["tanh_ready"], q + 1)
                nc.vector.tensor_scalar(num[:], th[:], 1.0, None, ALU.add).then_inc(S["e_num"], 1)
                nc.vector.tensor_scalar(den[:], th[:], -1.0, 1.0, ALU.mult, ALU.add).then_inc(S["e_den"], 1)
                dve.wait_ge(S["e_den"], q + 1)
                nc.vector.reciprocal(rden[:], den[:]).then_inc(S["e_rden"], 1)
                dve.wait_ge(S["e_num"], q + 1)
                dve.wait_ge(S["e_rden"], q + 1)
                nc.vector.tensor_tensor(ex[:], num[:], rden[:], ALU.mult).then_inc(S["e_exp"], 1)
                dve.wait_ge(S["e_exp"], q + 1)
                nc.vector.tensor_reduce(sm[:], ex[:], AX.X, ALU.add).then_inc(S["e_sum"], 1)
                dve.wait_ge(S["e_sum"], q + 1)
                nc.vector.reciprocal(rsm[:], sm[:]).then_inc(S["e_rsum"], 1)
                dve.wait_ge(S["prefix_out"], q + 1)
                nc.vector.tensor_tensor(
                    pe_[:].rearrange("p (j k) e -> p j k e", k=K), oh[:].rearrange("p (j k) e -> p j k e", k=K),
                    bc(bank[2][:, 0:GT * E].rearrange("p (j e) -> p j e", j=GT), 2, K),
                    ALU.mult).then_inc(S["pos_part"], 1)
                dve.wait_ge(S["pos_part"], q + 1)
                nc.vector.tensor_copy(seen[:, 0, :], seen[:, GT, :]).then_inc(S["seen_ready"], 1)
                nc.vector.tensor_reduce(pos[:], pe_[:], AX.X, ALU.add).then_inc(S["pos_ready"], 1)
                dve.wait_ge(S["pos_ready"], q + 1)
                nc.vector.tensor_scalar(far[:], pos[:], float(CAP), float(FAR), ALU.is_ge, ALU.mult).then_inc(S["far_ready"], 1)
                nc.vector.scalar_tensor_tensor(out=slot0[:], in0=eif[:].rearrange("p j k -> p (j k)"), scalar=float(CAP),
                                               in1=pos[:], op0=ALU.mult, op1=ALU.add).then_inc(S["slot_half"], 1)
                dve.wait_ge(S["far_ready"], q + 1)
                dve.wait_ge(S["slot_half"], q + 1)
                dve.wait_ge(S["rows_free"], q + AHEAD)
                nc.vector.tensor_tensor(slot[:], slot0[:], far[:], ALU.add).then_inc(S["slot_ready"], 1)
                dve.wait_ge(S["e_rsum"], q + 1)
                nc.vector.scalar_tensor_tensor(out=rows[:, :, :, D], in0=ex[:], scalar=0.5,
                                                   in1=rsm[:].unsqueeze(2).to_broadcast([P, GT, K]),
                                                   op0=ALU.mult, op1=ALU.mult)
                nc.vector.tensor_copy(rows[:].bitcast(U32)[:, :, :, D + 1],
                                      plc[:, bass.ds(g * (GT * K), GT * K)].rearrange("p (j k) -> p j k", j=GT)
                                      ).then_inc(S["rows_gate"], 1)

            def shared(q, g):
                dve.wait_ge(S["gates_up"], q + 1 + AHEAD)
                for c in range(HC):
                    dve.wait_ge(S["shared_gate"], HC * q + c + 1)
                    nc.vector.tensor_tensor(hs[:, c, :], gs[:, c, :], bank[5 + c][:], ALU.mult).then_inc(S["shared_hidden"], 1)
                dve.wait_ge(S["shared_out"], q + 1)
                xr = xres_of(g)
                nc.vector.scalar_tensor_tensor(out=xr.rearrange("p j d -> p (j d)"), in0=bank[7][:], scalar=0.5,
                                               in1=xr.rearrange("p j d -> p (j d)"), op0=ALU.mult,
                                               op1=ALU.add).then_inc(S["base_ready"], 1)

            def experts(f):
                with dve.Fori(0, E // 2) as i:
                    for b in range(2):
                        e = E * f + 2 * i + b
                        dve.wait_ge(S["e_gate_act"], e + 1)
                        dve.wait_ge(S["e_up_out"], e + 1)
                        for c in range(HC):
                            m = nc.vector.tensor_tensor(eh[b][:, c, :], eg[:, c, :], bank[3 + c][:, 0:CAP], ALU.mult)
                        m.then_inc(S["e_hidden"], 1)

            def combine(f, g):
                n = GROUPS * f + g
                dve.wait_ge(S["yk_in"], 16 * (n + 1))
                nc.vector.tensor_tensor(y2[:], yk[:, :, 0:2 * D], yk[:, :, 2 * D:], ALU.add).then_inc(S["y_pairs"], 1)
                dve.wait_ge(S["y_pairs"], n + 1 + AHEAD)
                nc.vector.tensor_tensor(y1[:], y2[:, :, 0:D], y2[:, :, D:], ALU.add).then_inc(S["y_sum"], 1)
                dve.wait_ge(S["y_sum"], n + 1)
                dve.wait_ge(S["base_ready"], GROUPS * (f + 1))
                xr = xres_of(g)
                nc.vector.tensor_tensor(xr, xr, y1[:], ALU.add).then_inc(S["x1_ready"], 1)

            def bias_rope(g, j):
                t = GT * g + j
                b = j % 2
                dve.wait_ge(S["qkv_out"], t + 1)
                nc.vector.tensor_tensor(qkv[b][:], bank[1][:, 0:3 * D], b_qkv[:], ALU.add).then_inc(S["qkv_biased"], 1)
                dve.wait_ge(S["qkv_biased"], t + 1 + AHEAD)
                v = qkv[b][:, 0:2 * D].rearrange("p (h e) -> p h e", e=DH)
                cs = cst[:, bass.ds(t * DH + C_COS, DH)]
                sn = cst[:, bass.ds(t * DH + C_SIN, DH)]
                hf = DH // 2
                nc.vector.tensor_tensor(rc[:], v, bc(cs, 1, 2 * HEADS), ALU.mult)
                nc.vector.tensor_tensor(rr[:, :, 0:hf], v[:, :, hf:], bc(sn[:, 0:hf], 1, 2 * HEADS), ALU.mult)
                nc.vector.tensor_tensor(rr[:, :, hf:], v[:, :, 0:hf], bc(sn[:, hf:], 1, 2 * HEADS),
                                        ALU.mult).then_inc(S["rope_parts"], 1)
                dve.wait_ge(S["rope_parts"], t + 1)
                nc.vector.tensor_tensor(qk[b][:], rc[:].rearrange("p h e -> p (h e)"), rr[:].rearrange("p h e -> p (h e)"),
                                        ALU.add).then_inc(S["rope_ready"], 1)

            def attention(g):
                bias_rope(g, 0)
                for j in range(GT):
                    t = GT * g + j
                    b = j % 2
                    dve.wait_ge(S["qkT_ready"], t + 1 + AHEAD)
                    nc.vector.tensor_tensor(qx[:], bc(qkT[b][:, 0:P], 1, HB), bc(head_mask, 2, P),
                                            ALU.mult).then_inc(S["qx_ready"], 1)
                    for h in range(4):
                        dve.wait_ge(S["score_out"], 4 * t + h + 1)
                        nc.vector.tensor_tensor(pr[:, h, :].rearrange("p (h t) -> p h t", h=HB),
                                                bank[4 + h][:].rearrange("p (h t) -> p h t", h=HB),
                                                bc(tri, 1, HB), ALU.mult).then_inc(S["masked"], 1)
                    if j + 1 < GT:
                        bias_rope(g, j + 1)
                    dve.wait_ge(S["kv_out"], t + 1)
                    nc.vector.tensor_tensor(kvm[:], bank[0][:, 0:D], block_mask, ALU.mult).then_inc(S["kv_masked"], 1)
                    dve.wait_ge(S["attn_out"], t + 1)
                    xj = xres[:, bass.ds(t * D, D)]
                    nc.vector.tensor_tensor(xj, xj, bank[3][:, 0:D], ALU.add).then_inc(S["x2_ready"], 1)
                    dve.wait_ge(S["kv_masked"], t + 1 + AHEAD)
                    nc.vector.tensor_tensor(state[:], state[:], kvm[:], ALU.add).then_inc(S["state_ready"], 1)

            for name in ("shared_hidden", "qkv_biased", "kv_masked", "masked", "x2_ready", "state_ready", "y_pairs", "seen_ready"):
                dve.sem_inc(S[name], AHEAD)
            nc.vector.memset(empty[:], 0.0).then_inc(S["empty_set"], 1)
            nc.vector.memset(zeros[:], 0.0).then_inc(S["empty_set"], 1)
            nc.vector.memset(seen[:], 0.0).then_inc(S["empty_set"], 1)
            nc.vector.memset(state[:], 0.0).then_inc(S["empty_set"], 1)
            dve.wait_ge(S["empty_set"], 4)
            nc.vector.memset(empty[:].bitcast(U32).rearrange("p (n r) -> p n r", r=ROW)[:, :, D + 1], FAR).then_inc(S["empty_set"], 1)
            dve.wait_ge(S["cen_in"], 16)
            nc.vector.tensor_tensor_reduce(cen_sq[:], cen[:], cen[:], 1.0, 0.0, ALU.mult, ALU.add,
                                           cen_n[:, 0:1]).then_inc(S["cen_square"], 1)
            dve.wait_ge(S["cen_root"], 1)
            nc.vector.tensor_scalar(cen_n[:, 2:3], cen_n[:, 1:2], 1e-12, None, ALU.max).then_inc(S["cen_inv0"], 1)
            dve.wait_ge(S["cen_inv0"], 1)
            nc.vector.reciprocal(cen_n[:, 3:4], cen_n[:, 2:3]).then_inc(S["cen_inv"], 1)
            dve.wait_ge(S["cen_inv"], 1)
            nc.vector.tensor_scalar(cen_sq[:], cen[:], cen_n[:, 3:4], None, ALU.mult).then_inc(S["cen_scaled"], 1)
            dve.wait_ge(S["cen_turned"], 1)
            nc.vector.tensor_copy(cenT[:], bank[2][:, 0:NG + E]).then_inc(S["cenT_ready"], 1)
            dve.wait_ge(S["consts_in"], 32)
            dve.wait_ge(S["small_in"], 16 * 5)
            dve.wait_ge(S["x_in"], 16)

            with dve.Fori(0, GROUPS) as g:
                n = q = g
                dve.wait_ge(S["xf_turned"], n + AHEAD)
                dve.wait_ge(S["rows_x"], q + AHEAD)
                dve.sem_inc(passed["dve"], 1)
                norm(n, g)
                route(q, n, g)
                shared(q, g)
            experts(0)
            dve.wait_ge(S["seen_ready"], (GT + 1) * GROUPS + AHEAD)
            nc.vector.memset(seen[:, 0, :], 0.0).then_inc(S["empty_set"], 1)
            dve.wait_ge(S["empty_set"], 6)
            with dve.Fori(0, GROUPS) as g:
                q = GROUPS + g
                combine(0, g)
                n = GROUPS + 2 * g
                dve.wait_ge(S["x1_ready"], g + 1)
                dve.wait_ge(S["xf_turned"], n + AHEAD)
                dve.wait_ge(S["rows_x"], q + AHEAD)
                dve.sem_inc(passed["dve"], 1)
                norm(n, g)
                attention(g)
                n2 = n + 1
                dve.wait_ge(S["x2_ready"], GT * (g + 1) + AHEAD)
                dve.wait_ge(S["xf_turned"], n2 + AHEAD)
                dve.sem_inc(passed["dve"], 1)
                norm(n2, g)
                route(q, n2, g)
                shared(q, g)
            experts(1)
            with dve.Fori(0, GROUPS) as g:
                combine(1, g)

        @block.scalar
        def _(act):
            def roots(n):
                act.wait_ge(S["sq_ready"], n + 1)
                nc.scalar.activation(rs[:], sq[:], ACT.Sqrt).then_inc(S["roots"], 1)

            def turn(n):
                act.wait_ge(S["xf_turned"], n + 1 + AHEAD)
                nc.scalar.activation(xfT[:], bank[0][:], ACT.Copy).then_inc(S["xfT_ready"], 1)

            def route(q, n):
                act.wait_ge(S["xf_ready"], GT * (n + 1))
                for c in range(HC):
                    act.wait_ge(S["gates_up"], q + 1 + AHEAD)
                    act.wait_ge(S["shared_hidden"], HC * q + AHEAD)
                    nc.scalar.activation(gs[:, c, :], bank[3 + c][:], ACT.Silu).then_inc(S["shared_gate"], 1)
                act.wait_ge(S["delta"], q + 1)
                nc.scalar.activation(th[:], dlt[:], ACT.Tanh, scale=0.5).then_inc(S["tanh_ready"], 1)
                act.wait_ge(S["rows_free"], q + AHEAD)
                for j in range(GT):
                    i = nc.scalar.activation(rows[:, j, :, 0:D], bc(xf[:, j, :], 1, K), ACT.Copy)
                i.then_inc(S["rows_x"], 1)

            def turn_x(f, i, d):
                e = expert(f, i, d)
                act.wait_ge(S["x_turned"], e + 1)
                act.wait_ge(S["e_up_out"], e - 1 if d else E * f)
                nc.scalar.activation(xbT[d % 2][:], bank[0][:, 0:CAP], ACT.Copy).then_inc(S["xT_ready"], 1)

            def gate(f, i, d):
                e = expert(f, i, d)
                act.wait_ge(S["e_gate_out"], e + 1)
                act.wait_ge(S["e_hidden"], e)
                for c in range(HC):
                    a = nc.scalar.activation(eg[:, c, :], bank[1 + c][:, 0:CAP], ACT.Silu)
                a.then_inc(S["e_gate_act"], 1)

            def scale(f, i, d):
                e = expert(f, i, d)
                act.wait_ge(S["e_down"], e + 1)
                act.wait_ge(S["results_free"], e + AHEAD)
                for t, m in enumerate(SIZES):
                    a = nc.scalar.activation(eo[d % 2][0:m, t, :], bank[5 + d % 2][0:m, t * D:(t + 1) * D], ACT.Copy,
                                             scale=xb[d % XB][0:m, t, D:D + 1])
                a.then_inc(S["e_scaled"], 1)

            def experts(f):
                turn_x(f, 0, 0)
                turn_x(f, 0, 1)
                gate(f, 0, 0)

                def step(i, d):
                    if not (isinstance(i, int) and XB * i + d + 1 >= E):
                        turn_x(f, i, d + 1)
                    gate(f, i, d)
                    scale(f, i, d - 1)
                with act.Fori(0, E // XB - 1) as i:
                    for d in range(1, XB + 1):
                        step(i, d)
                for d in range(1, XB):
                    step(E // XB - 1, d)
                scale(f, E // XB - 1, XB - 1)

            for name in ("xfT_ready", "qkT_ready", "e_scaled", "rows_x"):
                act.sem_inc(S[name], AHEAD)
            act.wait_ge(S["cen_square"], 1)
            nc.scalar.activation(cen_n[:, 1:2], cen_n[:, 0:1], ACT.Sqrt).then_inc(S["cen_root"], 1)
            with act.Fori(0, GROUPS) as g:
                roots(g)
                act.wait_ge(S["gates_up"], g + AHEAD)
                turn(g)
                route(g, g)
            experts(0)
            with act.Fori(0, GROUPS) as g:
                n = GROUPS + 2 * g
                roots(n)
                act.wait_ge(S["gates_up"], GROUPS + g + AHEAD)
                turn(n)
                for j in range(GT):
                    t = GT * g + j
                    act.wait_ge(S["qk_turned"], t + 1)
                    nc.scalar.activation(qkT[j % 2][:], bank[2][:, 0:2 * P], ACT.Copy).then_inc(S["qkT_ready"], 1)
                roots(n + 1)
                act.wait_ge(S["qkv_out"], GT * (g + 1))
                turn(n + 1)
                route(GROUPS + g, n + 1)
            experts(1)

        @block.tensor
        def _(pe):
            def turn(n):
                pe.wait_ge(S["xfT_ready"], n + AHEAD)
                for j in range(GT):
                    pe.wait_ge(S["xf_ready"], GT * n + j + 1)
                    i = nc.tensor.transpose(bank[0][:, j * P:(j + 1) * P], xf[:, j, :], ident)
                i.then_inc(S["xf_turned"], 1)

            def route(q, n):
                pe.wait_ge(S["xfT_ready"], n + 1 + AHEAD)
                for j in range(GT):
                    w = NG + E
                    i = nc.tensor.matmul(bank[1][:, j * w:(j + 1) * w], xfT[:, j * P:(j + 1) * P], cenT[:],
                                         start=True, stop=True)
                i.then_inc(S["router_out"], 1)
                for c in range(2 * HC):
                    i = nc.tensor.matmul(bank[3 + c][:], w_sgu[:, c * P:(c + 1) * P], xfT[:], start=True, stop=True)
                i.then_inc(S["gates_up"], 1)
                prefix(q)
                for j in range(GT):
                    for c in range(HC):
                        pe.wait_ge(S["shared_hidden"], HC * q + HC + AHEAD)
                        i = nc.tensor.matmul(bank[7][:, j * D:(j + 1) * D], hs[:, c, j * P:(j + 1) * P],
                                             w_sd[:, c * D:(c + 1) * D], start=(c == 0), stop=(c == HC - 1))
                i.then_inc(S["shared_out"], 1)

            def prefix(q):
                pe.wait_ge(S["seen_ready"], (GT + 1) * q + GT + AHEAD)
                nc.tensor.matmul(bank[2][:, 0:GT * E], strict, cnt[:].rearrange("p j e -> p (j e)"), start=True, stop=False)
                nc.tensor.matmul(bank[2][:, 0:GT * E], ones, seen[:, 0:GT, :].rearrange("p j e -> p (j e)"),
                                 start=False, stop=True).then_inc(S["prefix_out"], 1)

            def turn_x(f, i, d):
                e = expert(f, i, d)
                pe.wait_ge(s_xb[d % XB], (i + (E // XB * f + d // XB + 1)) * 32)
                pe.wait_ge(S["xT_ready"], e)
                for t, m in enumerate(SIZES):
                    a = nc.tensor.transpose(bank[0][:, t * P:t * P + m], xb[d % XB][0:m, t, 0:D], ident[0:m, 0:m])
                a.then_inc(S["x_turned"], 1)

            def gate_up(f, i, d):
                e = expert(f, i, d)
                w = w_e[d % 2]
                pe.wait_ge(s_w[d % 2], (i * (XB // 2) + (E // 2 * f + d // 2 + 1)) * 16)
                pe.wait_ge(S["xT_ready"], e + 1)
                pe.wait_ge(S["e_gate_act"], e)
                for c in range(2 * HC):
                    if c == HC:
                        pe.wait_ge(S["e_hidden"], e)
                    a = nc.tensor.matmul(bank[1 + c][:, 0:CAP], w[:, c * P:(c + 1) * P], xbT[d % 2][:], start=True, stop=True)
                    if c == HC - 1:
                        a.then_inc(S["e_gate_out"], 1)
                a.then_inc(S["e_up_out"], 1)

            def down(f, i, d):
                e = expert(f, i, d)
                pe.wait_ge(S["e_hidden"], e + 1)
                pe.wait_ge(S["e_scaled"], e + AHEAD)
                for t, m in enumerate(SIZES):
                    for c in range(HC):
                        a = nc.tensor.matmul(bank[5 + d % 2][0:m, t * D:(t + 1) * D], eh[d % 2][:, c, t * P:t * P + m],
                                             w_e[d % 2][:, 2 * H + c * D:2 * H + (c + 1) * D],
                                             start=(c == 0), stop=(c == HC - 1))
                a.then_inc(S["e_down"], 1)

            def experts(f):
                turn_x(f, 0, 0)
                turn_x(f, 0, 1)
                gate_up(f, 0, 0)

                def step(i, d):
                    if not (isinstance(i, int) and XB * i + d + 1 >= E):
                        turn_x(f, i, d + 1)
                    gate_up(f, i, d)
                    down(f, i, d - 1)
                with pe.Fori(0, E // XB - 1) as i:
                    for d in range(1, XB + 1):
                        step(i, d)
                for d in range(1, XB):
                    step(E // XB - 1, d)
                down(f, E // XB - 1, XB - 1)

            def qkv_of(g, n, j):
                t = GT * g + j
                pe.wait_ge(S["qkv_biased"], t + AHEAD)
                i = nc.tensor.matmul(bank[1][:, 0:3 * D], xfT[:, j * P:(j + 1) * P], w_qkv[:], start=True, stop=True)
                i.then_inc(S["qkv_out"], 1)

            def attention(g, n):
                pe.wait_ge(S["xfT_ready"], n + 1 + AHEAD)
                qkv_of(g, n, 0)
                for j in range(GT):
                    t = GT * g + j
                    b = j % 2
                    pe.wait_ge(S["rope_ready"], t + 1)
                    pe.wait_ge(S["qkT_ready"], t + AHEAD)
                    nc.tensor.transpose(bank[2][:, 0:P], qk[b][:, 0:D], ident)
                    nc.tensor.transpose(bank[2][:, P:2 * P], qk[b][:, D:], ident).then_inc(S["qk_turned"], 1)
                    if j + 1 < GT:
                        qkv_of(g, n, j + 1)
                    pe.wait_ge(S["kv_masked"], t + AHEAD)
                    nc.tensor.matmul(bank[0][:, 0:D], qk[b][:, D:], qkv[b][:, 2 * D:], start=True,
                                     stop=True).then_inc(S["kv_out"], 1)
                    pe.wait_ge(S["qx_ready"], t + 1)
                    for h in range(4):
                        pe.wait_ge(S["masked"], 4 * t + AHEAD)
                        nc.tensor.matmul(bank[4 + h][:], qkT[b][32 * h:32 * h + 32, P:2 * P],
                                         qx[32 * h:32 * h + 32, :, :].rearrange("p h t -> p (h t)"), start=True,
                                         stop=True).then_inc(S["score_out"], 1)
                    pe.wait_ge(S["x2_ready"], t + AHEAD)
                    pe.wait_ge(S["state_ready"], t + AHEAD)
                    nc.tensor.matmul(bank[3][:, 0:D], qkT[b][:, 0:P], state[:], start=True, stop=True)
                    for h in range(HEADS):
                        if h % HB == 0:
                            pe.wait_ge(S["masked"], 4 * t + h // HB + 1 + AHEAD)
                        i = nc.tensor.matmul(bank[3][:, h * DH:(h + 1) * DH],
                                             pr[:, h // HB, (h % HB) * P:(h % HB + 1) * P],
                                             qkv[b][:, 2 * D + h * DH:2 * D + (h + 1) * DH],
                                             start=False, stop=True, skip_group_check=True)
                    i.then_inc(S["attn_out"], 1)

            for name in ("xf_turned", "gates_up"):
                pe.sem_inc(S[name], AHEAD)
            pe.wait_ge(S["consts_in"], 32)
            pe.wait_ge(S["empty_set"], 5)
            pe.wait_ge(S["cen_scaled"], 1)
            nc.tensor.transpose(bank[2][:, 0:NG + E], cen_sq[:], ident[0:NG + E, 0:NG + E]).then_inc(S["cen_turned"], 1)
            pe.wait_ge(S["cenT_ready"], 1)
            pe.wait_ge(S["small_in"], 16 * 5)
            with pe.Fori(0, GROUPS) as g:
                turn(g)
                route(g, g)
            pe.wait_ge(S["base_ready"], GROUPS)
            experts(0)
            pe.wait_ge(S["e_scaled"], E + AHEAD)
            with pe.Fori(0, GROUPS) as g:
                n = GROUPS + 2 * g
                turn(n)
                attention(g, n)
                turn(n + 1)
                pe.wait_ge(S["x2_ready"], GT * (g + 1) + AHEAD)
                route(GROUPS + g, n + 1)
            pe.wait_ge(S["base_ready"], 2 * GROUPS)
            experts(1)

        @block.gpsimd
        def _(pool):
            def dispatch(f, q):
                pool.wait_ge(S["rows_gate"], q + 1)
                pool.wait_ge(S["rows_x"], q + 1 + AHEAD)
                pool.sem_inc(passed["pool"], 1)
                for j in range(GT):
                    for k in range(K):
                        pool.indirect_dma_start(
                            slots[f], bass.IndirectOffsetOnAxis(ap=slot[:, j * K + k:j * K + k + 1], axis=0),
                            rows[:, j, k, :], None, bounds_check=last_slot, oob_is_err=False).then_inc(S["slots_sent"], 16)
                pool.wait_ge(S["slots_sent"], (q + 1) * (16 * GT * K))
                pool.sem_inc(S["rows_free"], 1)

            def results(f, i, d):
                pool.wait_ge(S["e_scaled"], expert(f, i, d) + 1 + AHEAD)
                pool.sem_inc(passed["pool"], 1)
                for t, m in enumerate(SIZES):
                    pool.indirect_dma_start(
                        routed[f], bass.IndirectOffsetOnAxis(ap=xb[d][:].bitcast(U32)[0:m, t, D + 1:D + 2], axis=0),
                        eo[d % 2][0:m, t, :], None, bounds_check=last_place, oob_is_err=False).then_inc(s_sc[d], 16)
                if not (f == 0 and isinstance(i, int) and d == 0):
                    pool.wait_ge(s_sc[(d - 1) % XB], sent_count(f, i, d - 1))
                    pool.sem_inc(S["results_free"], 1)

            for name in ("rows_free", "results_free"):
                pool.sem_inc(S[name], AHEAD * (2 if name == "results_free" else 1))
            last_slot = pool.to_reg(SLOTS - 1)
            last_place = pool.to_reg(TOKENS * K - 1)
            pool.wait_ge(S["empty_sent0"], 16 * 8)
            with pool.Fori(0, GROUPS) as g:
                dispatch(0, g)
            pool.wait_ge(S["zeros_sent0"], 16 * 4)
            for d in range(XB):
                results(0, 0, d)
            with pool.Fori(1, E // XB) as i:
                for d in range(XB):
                    results(0, i, d)
            pool.wait_ge(S["empty_sent1"], 16 * 8)
            with pool.Fori(0, GROUPS) as g:
                dispatch(1, GROUPS + g)
            pool.wait_ge(S["zeros_sent1"], 16 * 4)
            for d in range(XB):
                results(1, 0, d)
            with pool.Fori(1, E // XB) as i:
                for d in range(XB):
                    results(1, i, d)

        @block.sync
        def _(sp):
            def load_weights(b, e):
                sp.dma_start(w_e[b][:], ew[bass.ds(e, 1), :, :].rearrange("e p n -> (e p) n")).then_inc(s_w[b], 16)

            def load_slots(f, b, e):
                src = slots[f]
                sp.dma_start(xb[b][:, 0:FULL, :], src[bass.ds(e * CAP, FULL * P), :].rearrange("(t p) r -> p t r", p=P)
                             ).then_inc(s_xb[b], 16)
                sp.dma_start(xb[b][0:REST, FULL, :], src[bass.ds(e * CAP + FULL * P, REST), :]).then_inc(s_xb[b], 16)

            def fill(f):
                a = slots[f].rearrange("(c p n) r -> c p (n r)", p=P, n=10)
                z = routed[f].rearrange("(c p n) d -> c p (n d)", p=P, n=16)
                for c in range(SLOTS // (10 * P)):
                    sp.dma_start(a[c], empty[:]).then_inc(S[f"empty_sent{f}"], 16)
                for c in range(TOKENS * K // (16 * P)):
                    sp.dma_start(z[c], zeros[:]).then_inc(S[f"zeros_sent{f}"], 16)

            sp.dma_start(cen[:], cents).then_inc(S["cen_in"], 16)
            sp.dma_start(cst[:], consts).then_inc(S["consts_in"], 16)
            sp.dma_start(plc[:], places).then_inc(S["consts_in"], 16)
            sp.dma_start(xres[:].rearrange("p (t d) -> p t d", t=TILES), x_t).then_inc(S["x_in"], 16)
            sp.dma_start(w_sgu[:], sgu).then_inc(S["small_in"], 16)
            sp.dma_start(w_sd[:].rearrange("p (c d) -> p c d", c=HC), sd.rearrange("(c p) d -> p c d", p=P)).then_inc(S["small_in"], 16)
            sp.dma_start(w_qkv[:], wqkv).then_inc(S["small_in"], 16)
            sp.dma_start(b_qkv[:], bqkv.to_broadcast([P, 3 * D])).then_inc(S["small_in"], 16)
            sp.dma_start(e_bias[:], ebias.to_broadcast([P, E])).then_inc(S["small_in"], 16)
            sp.wait_ge(S["empty_set"], 5)
            fill(0)
            fill(1)
            for f in range(2):
                load_weights(0, 0)
                load_weights(1, 1)
                sp.wait_ge(S["slots_sent"], 16 * K * TILES * (f + 1))
                for d in range(XB):
                    load_slots(f, d, d)

                def step(i, d):
                    if not (isinstance(i, int) and XB * i + d + 2 >= E):
                        sp.wait_ge(S["e_down"], expert(f, i, d) + 1)
                        load_weights(d % 2, expert(0, i, d) + 2)
                    if not isinstance(i, int):
                        sp.wait_ge(s_sc[d], sent_count(f, i, d))
                        load_slots(f, d, expert(0, i, d) + XB)
                with sp.Fori(0, E // XB - 1) as i:
                    for d in range(XB):
                        step(i, d)
                for d in range(2):
                    step(E // XB - 1, d)
                for d in range(XB):
                    sp.wait_ge(s_sc[d], 16 * ST * (E // XB) * (f + 1))
                with sp.Fori(0, GROUPS) as g:
                    sp.wait_ge(S["y_pairs"], g + GROUPS * f + AHEAD)
                    sp.dma_start(yk[:], routed[f][bass.ds(g * (GW * K), GW * K), :].rearrange("(j p k) d -> p j (k d)", p=P, k=K)
                                 ).then_inc(S["yk_in"], 16)
                    if f:
                        sp.wait_ge(S["x1_ready"], g + (GROUPS + 1))
                        sp.dma_start(out_t[:, bass.ds(g * GT, GT), :], xres_of(g)).then_inc(S["out_sent"], 16)
            sp.wait_ge(S["out_sent"], 16 * GROUPS)


def kernel(L0_attn_x, L0_attn_W_qkv, L0_attn_b_qkv, L0_ffn_group_centroids, L0_ffn_expert_centroids, L0_ffn_bias,
           L0_ffn_wg, L0_ffn_wu, L0_ffn_wd, L0_ffn_sg, L0_ffn_su, L0_ffn_sd):
    import concourse.bacc as bacc
    from concourse.bass_utils import run_bass_kernel_spmd

    n = np.asarray
    consts, places = shape_constants()
    wd = n(L0_ffn_wd).reshape(E, HC, P, D).transpose(0, 2, 1, 3).reshape(E, P, HC * D)
    ins = {
        "x": n(L0_attn_x).reshape(TOKENS, D),
        "consts": consts,
        "places": places,
        "wqkv": n(L0_attn_W_qkv).T,
        "bqkv": n(L0_attn_b_qkv).reshape(1, 3 * D),
        "cents": np.concatenate([n(L0_ffn_group_centroids), n(L0_ffn_expert_centroids)], 0),
        "ebias": n(L0_ffn_bias).reshape(1, E),
        "ew": np.concatenate([n(L0_ffn_wg), n(L0_ffn_wu), wd], 2),
        "sgu": np.concatenate([n(L0_ffn_sg), n(L0_ffn_su)], 1),
        "sd": n(L0_ffn_sd),
    }
    ins = {k: np.ascontiguousarray(v) for k, v in ins.items()}
    nc = bacc.Bacc("TRN2", target_bir_lowering=False, num_devices=1)
    args = {k: nc.dram_tensor(k, v.shape, mybir.dt.from_np(v.dtype), kind="ExternalInput").ap() for k, v in ins.items()}
    args["out"] = nc.dram_tensor("out", (TOKENS, D), F32, kind="ExternalOutput").ap()
    macaron(nc, **args)
    r = run_bass_kernel_spmd(nc, [ins], core_ids=[0])
    return r.results[0]["out"].reshape(1, TOKENS, D)
```

```python
from contextlib import ExitStack

import numpy as np

import concourse.bass as bass
from concourse import mybir

F32 = mybir.dt.float32
U32 = mybir.dt.uint32
ALU = mybir.AluOpType
ACT = mybir.ActivationFunctionType
AX = mybir.AxisListType

P = 128
D = 128
TOKENS = 2048
TILES = TOKENS // P
GT = 4
GROUPS = TILES // GT
GW = GT * P
E = 32
NG = 8
EPG = E // NG
K = 4
H = 256
HC = H // P
CAP = max(1, int(TOKENS / E * K * 1.25))
FULL = CAP // P
REST = CAP - FULL * P
ST = FULL + 1
SLOTS = E * CAP
FAR = 1 << 16
ROW = D + 2
HEADS = 16
DH = D // HEADS
HB = 4
ROPE_BASE = 10000.0
LN_EPS = 1e-5
SIZES = [P] * FULL + [REST]
FILLS = 8
XB = 8
WB = 4

C_IDENT, C_TRI, C_STRICT, C_ONES, C_BLOCK = (i * P for i in range(5))
C_HEAD = 5 * P
C_IOTA = C_HEAD + HB
C_COS = C_IOTA + E
C_SIN = C_COS + TILES * DH
C_ALL = C_SIN + TILES * DH


def shape_constants():
    c = np.zeros((P, C_ALL), np.float32)
    i = np.arange(P)
    c[:, C_IDENT:C_IDENT + P] = i[:, None] == i[None, :]
    c[:, C_TRI:C_TRI + P] = i[:, None] <= i[None, :]
    c[:, C_STRICT:C_STRICT + P] = i[:, None] < i[None, :]
    c[:, C_ONES:C_ONES + P] = 1.0
    c[:, C_BLOCK:C_BLOCK + P] = i[:, None] // DH == i[None, :] // DH
    c[:, C_HEAD:C_HEAD + HB] = (i[:, None] // DH) % HB == np.arange(HB)[None, :]
    c[:, C_IOTA:C_IOTA + E] = np.arange(E)[None, :]
    freq = np.float32(1) / np.float32(ROPE_BASE) ** (np.arange(0, DH, 2, dtype=np.float32) / np.float32(DH))
    ang = np.arange(TOKENS, dtype=np.float32)[:, None] * freq[None, :]
    cos = np.concatenate([np.cos(ang), np.cos(ang)], 1)
    sin = np.concatenate([-np.sin(ang), np.sin(ang)], 1)
    for at, t in ((C_COS, cos), (C_SIN, sin)):
        c[:, at:at + TILES * DH] = t.reshape(TILES, P, DH).transpose(1, 0, 2).reshape(P, -1)
    place = (np.arange(TILES)[None, :, None] * P + i[:, None, None]) * K + np.arange(K)[None, None, :]
    return c, np.ascontiguousarray(place.reshape(P, TILES * K)).astype(np.uint32)


def macaron(nc, x, consts, places, wqkv, bqkv, cents, ebias, ew, sgu, sd, out):
    x_t = x.rearrange("(t p) d -> p t d", p=P)
    out_t = out.rearrange("(t p) d -> p t d", p=P)

    with ExitStack() as ctx:
        def sb(name, shape, dt=F32):
            return ctx.enter_context(nc.sbuf_tensor(name, shape, dt))

        def sem(name):
            return ctx.enter_context(nc.semaphore(name))

        slots = [nc.dram_tensor(f"slots{f}", [SLOTS, ROW], F32, kind="Internal").ap() for f in range(2)]
        routed = [nc.dram_tensor(f"routed{f}", [TOKENS * K, D], F32, kind="Internal").ap() for f in range(2)]

        bank = [ctx.enter_context(nc.psum_tensor(f"bank{i}", [P, 512], F32)) for i in range(8)]

        cst = sb("cst", [P, C_ALL])
        plc = sb("plc", [P, TILES * K], U32)
        w_qkv = sb("w_qkv", [P, 3 * D])
        b_qkv = sb("b_qkv", [P, 3 * D])
        cen = sb("cen", [NG + E, D])
        cen_sq = sb("cen_sq", [NG + E, D])
        cen_n = sb("cen_n", [NG + E, 4])
        cenT = sb("cenT", [P, P])
        e_bias = sb("e_bias", [P, E])
        w_sgu = sb("w_sgu", [P, 2 * H])
        w_sd = sb("w_sd", [P, HC * D])
        zeros = sb("zeros", [P, 8 * D])
        empty = sb("empty", [P, 10 * ROW])

        xres = sb("xres", [P, TILES * D])
        st = {k: sb(f"st_{k}", [P, GT, 6]) for k in "af"}
        mv = {k: sb(f"mv_{k}", [P, GT, 2]) for k in "af"}
        ve = {k: sb(f"ve_{k}", [P, GT]) for k in "af"}
        sq = {k: sb(f"sq_{k}", [P, 2, GT]) for k in "af"}
        rs = {k: sb(f"rs_{k}", [P, 2, GT]) for k in "af"}
        xf = {k: sb(f"xf_{k}", [P, GT, D]) for k in "af"}
        xfT = {k: sb(f"xfT_{k}", [P, GW]) for k in "af"}
        rn0 = sb("rn0", [P, GT])
        rn = sb("rn", [P, GT])

        gs = sb("gs", [P, HC, GW])
        hs = sb("hs", [P, HC, GW])
        sc = sb("sc", [P, GT, NG + E])
        es = sb("es", [P, GT, E])
        g8 = sb("g8", [P, GT, 8])
        gi8 = sb("gi8", [P, GT, 8], U32)
        gif = sb("gif", [P, GT, K])
        geq = sb("geq", [P, GT * K, NG])
        gm = sb("gm", [P, GT, NG])
        pen = sb("pen", [P, GT, NG])
        mk0 = sb("mk0", [P, GT * NG, EPG])
        mk = sb("mk", [P, GT * NG, EPG])
        v8 = sb("v8", [P, GT, 8])
        vi8 = sb("vi8", [P, GT, 8], U32)
        eif = sb("eif", [P, GT, K])
        dlt = sb("dlt", [P, GT, K])
        th = sb("th", [P, GT, K])
        num = sb("num", [P, GT, K])
        den = sb("den", [P, GT, K])
        rden = sb("rden", [P, GT, K])
        ex = sb("ex", [P, GT, K])
        sm = sb("sm", [P, GT])
        rsm = sb("rsm", [P, GT])
        oh = sb("oh", [P, GT * K, E])
        cnt = sb("cnt", [P, GT, E])
        seen = sb("seen", [P, GT + 1, E])
        pe_ = sb("pe_", [P, GT * K, E])
        pos = sb("pos", [P, GT * K])
        far = sb("far", [P, GT * K])
        slot0 = sb("slot0", [P, GT * K])
        slot = sb("slot", [P, GT * K], U32)
        rows = sb("rows", [P, GT, K, ROW])

        w_e = [sb(f"w_e{b}", [P, 3 * H]) for b in range(WB)]
        xb = [sb(f"xb{b}", [P, ST, ROW]) for b in range(XB)]
        xbT = [sb(f"xbT{b}", [P, CAP]) for b in range(2)]
        eg = sb("eg", [P, HC, CAP])
        eh = [sb(f"eh{b}", [P, HC, CAP]) for b in range(2)]
        eo = [sb(f"eo{b}", [P, ST, D]) for b in range(2)]

        yk = sb("yk", [P, GROUPS * GT * K * D])
        y2 = sb("y2", [P, GT, 2 * D])
        y1 = sb("y1", [P, GT, D])

        qkv = [sb(f"qkv{b}", [P, 3 * D]) for b in range(2)]
        rc = sb("rc", [P, 2 * HEADS, DH])
        rr = sb("rr", [P, 2 * HEADS, DH])
        qk = [sb(f"qk{b}", [P, 2 * D]) for b in range(2)]
        qkT = [sb(f"qkT{b}", [P, 2 * P]) for b in range(2)]
        qx = sb("qx", [P, HB, P])
        pr = sb("pr", [P, HB, 4 * P])
        vp = [sb(f"vp{b}", [P, HEADS * (D + DH)]) for b in range(2)]
        oT = sb("oT", [P, P])
        kvm = sb("kvm", [P, D])
        state = sb("state", [P, D])

        ident = cst[:, C_IDENT:C_IDENT + P]
        tri = cst[:, C_TRI:C_TRI + P]
        strict = cst[:, C_STRICT:C_STRICT + P]
        ones = cst[:, C_ONES:C_ONES + P]
        block_mask = cst[:, C_BLOCK:C_BLOCK + P]
        head_mask = cst[:, C_HEAD:C_HEAD + HB]
        iota = cst[:, C_IOTA:C_IOTA + E]

        names = """consts_in small_in x_in empty_set empty_sent0 zeros_sent0 slots_sent routed_sent
            empty_sent1 zeros_sent1 cen_in cen_square cen_root cen_inv0 cen_inv cen_scaled cen_turned cenT_ready
            stats_a mean_var_a var_eps_a var_inv_a sq_ready_a roots_a xf_ready_a xf_turned_a xfT_ready_a
            stats_f mean_var_f var_eps_f var_inv_f sq_ready_f roots_f xf_ready_f xf_turned_f xfT_ready_f
            norm_floor norm_inv router_out gates_up vp_ready state_read oT_out oT_ready shared_gate shared_hidden shared_out base_ready
            scores_n es_ready g_top g_idx g_idxf g_eq g_mask g_pen mk_half mk_ready v_top v_idx v_idxf
            delta tanh_ready e_num e_den e_rden e_exp e_sum e_rsum hot count seen_ready prefix_out
            rows_free results_free pos_part pos_ready far_ready slot_half slot_ready rows_x rows_gate
            x_turned xT_ready e_gate_out e_up_out e_gate_act e_hidden e_down e_scaled
            yk_in y_pairs y_sum x1_ready qkv_out qkv_biased rope_parts rope_ready qk_turned qkT_ready
            qx_ready score_out masked attn_out kv_out x2_ready kv_masked state_ready out_sent""".split()
        S = {n: sem(n) for n in names}
        passed = {e: sem(f"passed_{e}") for e in ("dve", "pool", "sp")}
        AHEAD = 1
        s_w = [sem(f"weights_in{b}") for b in range(WB)]
        s_xb = [sem(f"slots_in{b}") for b in range(XB)]
        s_sc = [sem(f"results_sent{b}") for b in range(XB)]

        block = ctx.enter_context(nc.Block())

        def bc(ap, axis, n):
            shape = list(ap.shape)
            shape.insert(axis, n)
            return ap.unsqueeze(axis).to_broadcast(shape)

        def expert(f, i, d):
            return XB * i + (E * f + d)

        def sent_count(f, i, d):
            return (i + (E // XB * f + d // XB + 1)) * (16 * ST)

        def xres_of(g):
            return xres[:, bass.ds(g * GW, GW)].rearrange("p (j d) -> p j d", j=GT)

        def ln_pass(f, g, second=True):
            return g if f == 0 else GROUPS + 2 * g + (1 if second else 0)

        @block.vector
        def _(dve):
            def norm(kind, n, g):
                xr = xres_of(g)
                for j in range(GT):
                    i = nc.vector.bn_stats(st[kind][:, j, :], xr[:, j, :])
                i.then_inc(S[f"stats_{kind}"], 1)
                dve.wait_ge(S[f"stats_{kind}"], n + 1)
                dve.sem_inc(passed["dve"], 1)
                for j in range(GT):
                    i = nc.vector.bn_aggr(mv[kind][:, j, :], st[kind][:, j, :])
                i.then_inc(S[f"mean_var_{kind}"], 1)
                dve.wait_ge(S[f"mean_var_{kind}"], n + 1)
                nc.vector.tensor_scalar(ve[kind][:], mv[kind][:, :, 1], LN_EPS, None, ALU.add).then_inc(S[f"var_eps_{kind}"], 1)
                dve.wait_ge(S[f"var_eps_{kind}"], n + 1)
                nc.vector.reciprocal(sq[kind][:, 0, :], ve[kind][:]).then_inc(S[f"var_inv_{kind}"], 1)
                dve.wait_ge(S[f"var_inv_{kind}"], n + 1)
                nc.vector.scalar_tensor_tensor(out=sq[kind][:, 1, :], in0=mv[kind][:, :, 1], scalar=float(D),
                                               in1=sq[kind][:, 0, :], op0=ALU.mult,
                                               op1=ALU.mult).then_inc(S[f"sq_ready_{kind}"], 1)
                dve.wait_ge(S[f"roots_{kind}"], n + 1)
                for j in range(GT):
                    nc.vector.tensor_scalar(xf[kind][:, j, :], xr[:, j, :], mv[kind][:, j, 0:1], rs[kind][:, 0, j:j + 1],
                                            ALU.subtract, ALU.mult).then_inc(S[f"xf_ready_{kind}"], 1)

            def norm_f(q, g):
                dve.wait_ge(S["xf_turned_f"], q + AHEAD)
                dve.wait_ge(S["rows_x"], q + AHEAD)
                dve.sem_inc(passed["dve"], 1)
                norm("f", q, g)
                nc.vector.tensor_scalar(rn0[:], rs["f"][:, 1, :], 1e-12, None, ALU.max).then_inc(S["norm_floor"], 1)
                dve.wait_ge(S["norm_floor"], q + 1)
                nc.vector.reciprocal(rn[:], rn0[:]).then_inc(S["norm_inv"], 1)

            def route_experts(q):
                dve.wait_ge(S["norm_inv"], q + 1)
                dve.wait_ge(S["router_out"], q + 1)
                nc.vector.tensor_tensor(sc[:], bank[6][:].rearrange("p (j e) -> p j e", j=GT)[:, :, 0:NG + E],
                                        bc(rn[:], 2, NG + E), ALU.mult).then_inc(S["scores_n"], 1)
                dve.wait_ge(S["scores_n"], q + 1)
                nc.vector.tensor_tensor(es[:], sc[:, :, NG:], bc(e_bias[:], 1, GT), ALU.add).then_inc(S["es_ready"], 1)
                for j in range(GT):
                    i = nc.vector.max(g8[:, j, :], sc[:, j, 0:NG])
                i.then_inc(S["g_top"], 1)
                dve.wait_ge(S["g_top"], q + 1)
                dve.sem_inc(passed["dve"], 1)
                for j in range(GT):
                    i = nc.vector.max_index(gi8[:, j, :], g8[:, j, :], sc[:, j, 0:NG])
                i.then_inc(S["g_idx"], 1)
                dve.wait_ge(S["g_idx"], q + 1)
                nc.vector.tensor_copy(gif[:], gi8[:, :, 0:K]).then_inc(S["g_idxf"], 1)
                dve.wait_ge(S["g_idxf"], q + 1)
                nc.vector.tensor_tensor(geq[:], bc(gif[:].rearrange("p j k -> p (j k)"), 2, NG),
                                        bc(iota[:, 0:NG], 1, GT * K), ALU.is_equal).then_inc(S["g_eq"], 1)
                dve.wait_ge(S["g_eq"], q + 1)
                nc.vector.tensor_reduce(gm[:], geq[:].rearrange("p (j k) g -> p j g k", k=K), AX.X,
                                        ALU.add).then_inc(S["g_mask"], 1)
                dve.wait_ge(S["g_mask"], q + 1)
                nc.vector.tensor_scalar(pen[:], gm[:], 1e9, -1e9, ALU.mult, ALU.add).then_inc(S["g_pen"], 1)
                dve.wait_ge(S["es_ready"], q + 1)
                nc.vector.tensor_tensor(mk0[:], es[:].rearrange("p j (g e) -> p (j g) e", e=EPG),
                                        bc(gm[:].rearrange("p j g -> p (j g)"), 2, EPG), ALU.mult).then_inc(S["mk_half"], 1)
                dve.wait_ge(S["mk_half"], q + 1)
                dve.wait_ge(S["g_pen"], q + 1)
                nc.vector.tensor_tensor(mk[:], mk0[:], bc(pen[:].rearrange("p j g -> p (j g)"), 2, EPG),
                                        ALU.add).then_inc(S["mk_ready"], 1)
                dve.wait_ge(S["mk_ready"], q + 1)
                dve.sem_inc(passed["dve"], 1)
                mkj = mk[:].rearrange("p (j g) e -> p j (g e)", j=GT)
                for j in range(GT):
                    i = nc.vector.max(v8[:, j, :], mkj[:, j, :])
                i.then_inc(S["v_top"], 1)
                dve.wait_ge(S["v_top"], q + 1)
                dve.sem_inc(passed["dve"], 1)
                for j in range(GT):
                    i = nc.vector.max_index(vi8[:, j, :], v8[:, j, :], mkj[:, j, :])
                i.then_inc(S["v_idx"], 1)
                nc.vector.tensor_tensor(dlt[:], v8[:, :, 0:K], v8[:, :, 0:1].to_broadcast([P, GT, K]),
                                        ALU.subtract).then_inc(S["delta"], 1)

            def route_counts(q):
                dve.wait_ge(S["v_idx"], q + 1)
                nc.vector.tensor_copy(eif[:], vi8[:, :, 0:K]).then_inc(S["v_idxf"], 1)
                dve.wait_ge(S["v_idxf"], q + 1)
                nc.vector.tensor_tensor(oh[:], bc(eif[:].rearrange("p j k -> p (j k)"), 2, E),
                                        bc(iota, 1, GT * K), ALU.is_equal).then_inc(S["hot"], 1)
                dve.wait_ge(S["hot"], q + 1)
                nc.vector.tensor_reduce(cnt[:], oh[:].rearrange("p (j k) e -> p j e k", k=K), AX.X,
                                        ALU.add).then_inc(S["count"], 1)
                dve.wait_ge(S["count"], q + 1)
                dve.wait_ge(S["seen_ready"], (GT + 1) * q + AHEAD)
                for j in range(GT):
                    nc.vector.tensor_tensor(seen[:, j + 1, :], seen[:, j, :], cnt[:, j, :],
                                            ALU.add).then_inc(S["seen_ready"], 1)
                    dve.wait_ge(S["seen_ready"], (GT + 1) * q + j + 1 + AHEAD)

            def shared_hidden(q, c):
                dve.wait_ge(S["gates_up"], HC * q + c + 1 + AHEAD)
                dve.wait_ge(S["shared_gate"], HC * q + c + 1)
                nc.vector.tensor_tensor(hs[:, c, :], gs[:, c, :], bank[7][:], ALU.mult).then_inc(S["shared_hidden"], 1)

            def route_slots(q, g):
                dve.wait_ge(S["tanh_ready"], q + 1)
                nc.vector.tensor_scalar(num[:], th[:], 1.0, None, ALU.add).then_inc(S["e_num"], 1)
                nc.vector.tensor_scalar(den[:], th[:], -1.0, 1.0, ALU.mult, ALU.add).then_inc(S["e_den"], 1)
                dve.wait_ge(S["e_den"], q + 1)
                nc.vector.reciprocal(rden[:], den[:]).then_inc(S["e_rden"], 1)
                dve.wait_ge(S["e_num"], q + 1)
                dve.wait_ge(S["e_rden"], q + 1)
                nc.vector.tensor_tensor(ex[:], num[:], rden[:], ALU.mult).then_inc(S["e_exp"], 1)
                dve.wait_ge(S["e_exp"], q + 1)
                nc.vector.tensor_reduce(sm[:], ex[:], AX.X, ALU.add).then_inc(S["e_sum"], 1)
                dve.wait_ge(S["e_sum"], q + 1)
                nc.vector.reciprocal(rsm[:], sm[:]).then_inc(S["e_rsum"], 1)
                dve.wait_ge(S["prefix_out"], q + 1)
                nc.vector.tensor_tensor(
                    pe_[:].rearrange("p (j k) e -> p j k e", k=K), oh[:].rearrange("p (j k) e -> p j k e", k=K),
                    bc(bank[6][:, 0:GT * E].rearrange("p (j e) -> p j e", j=GT), 2, K),
                    ALU.mult).then_inc(S["pos_part"], 1)
                dve.wait_ge(S["pos_part"], q + 1)
                nc.vector.tensor_copy(seen[:, 0, :], seen[:, GT, :]).then_inc(S["seen_ready"], 1)
                nc.vector.tensor_reduce(pos[:], pe_[:], AX.X, ALU.add).then_inc(S["pos_ready"], 1)
                dve.wait_ge(S["pos_ready"], q + 1)
                nc.vector.tensor_scalar(far[:], pos[:], float(CAP), float(FAR), ALU.is_ge, ALU.mult).then_inc(S["far_ready"], 1)
                nc.vector.scalar_tensor_tensor(out=slot0[:], in0=eif[:].rearrange("p j k -> p (j k)"), scalar=float(CAP),
                                               in1=pos[:], op0=ALU.mult, op1=ALU.add).then_inc(S["slot_half"], 1)
                dve.wait_ge(S["far_ready"], q + 1)
                dve.wait_ge(S["slot_half"], q + 1)
                dve.wait_ge(S["rows_free"], q + AHEAD)
                nc.vector.tensor_tensor(slot[:], slot0[:], far[:], ALU.add).then_inc(S["slot_ready"], 1)
                dve.wait_ge(S["e_rsum"], q + 1)
                nc.vector.scalar_tensor_tensor(out=rows[:, :, :, D], in0=ex[:], scalar=0.5,
                                                   in1=rsm[:].unsqueeze(2).to_broadcast([P, GT, K]),
                                                   op0=ALU.mult, op1=ALU.mult)
                nc.vector.tensor_copy(rows[:].bitcast(U32)[:, :, :, D + 1],
                                      plc[:, bass.ds(g * (GT * K), GT * K)].rearrange("p (j k) -> p j k", j=GT)
                                      ).then_inc(S["rows_gate"], 1)

            def shared_out(q, g):
                dve.wait_ge(S["shared_out"], q + 1)
                xr = xres_of(g)
                nc.vector.scalar_tensor_tensor(out=xr.rearrange("p j d -> p (j d)"), in0=bank[7][:], scalar=0.5,
                                               in1=xr.rearrange("p j d -> p (j d)"), op0=ALU.mult,
                                               op1=ALU.add).then_inc(S["base_ready"], 1)

            def feed_forward(q, g):
                norm_f(q, g)
                route_experts(q)
                route_counts(q)
                shared_hidden(q, 0)
                shared_hidden(q, 1)
                route_slots(q, g)
                shared_out(q, g)

            def experts(f):
                with dve.Fori(0, E // 2) as i:
                    for b in range(2):
                        e = E * f + 2 * i + b
                        dve.wait_ge(S["e_gate_act"], e + 1)
                        dve.wait_ge(S["e_up_out"], e + 1)
                        for c in range(HC):
                            m = nc.vector.tensor_tensor(eh[b][:, c, :], eg[:, c, :], bank[3 + c][:, 0:CAP], ALU.mult)
                        m.then_inc(S["e_hidden"], 1)

            def combine(f, g):
                n = GROUPS * f + g
                dve.wait_ge(S["yk_in"], 16 * (n + 1))
                y = yk[:, bass.ds(g * (GW * K), GW * K)].rearrange("p (j k) -> p j k", j=GT)
                nc.vector.tensor_tensor(y2[:], y[:, :, 0:2 * D], y[:, :, 2 * D:], ALU.add).then_inc(S["y_pairs"], 1)
                dve.wait_ge(S["y_pairs"], n + 1)
                nc.vector.tensor_tensor(y1[:], y2[:, :, 0:D], y2[:, :, D:], ALU.add).then_inc(S["y_sum"], 1)
                dve.wait_ge(S["y_sum"], n + 1)
                dve.wait_ge(S["base_ready"], GROUPS * (f + 1))
                xr = xres_of(g)
                nc.vector.tensor_tensor(xr, xr, y1[:], ALU.add).then_inc(S["x1_ready"], 1)

            def bias_rope(g, j):
                t = GT * g + j
                b = j % 2
                dve.wait_ge(S["qkv_out"], t + 1 + AHEAD)
                nc.vector.tensor_tensor(qkv[b][:], bank[1][:, 0:3 * D], b_qkv[:], ALU.add).then_inc(S["qkv_biased"], 1)
                dve.wait_ge(S["qkv_biased"], t + 1 + AHEAD)
                v = qkv[b][:, 0:2 * D].rearrange("p (h e) -> p h e", e=DH)
                cs = cst[:, bass.ds(t * DH + C_COS, DH)]
                sn = cst[:, bass.ds(t * DH + C_SIN, DH)]
                hf = DH // 2
                nc.vector.tensor_tensor(rc[:], v, bc(cs, 1, 2 * HEADS), ALU.mult)
                nc.vector.tensor_tensor(rr[:, :, 0:hf], v[:, :, hf:], bc(sn[:, 0:hf], 1, 2 * HEADS), ALU.mult)
                nc.vector.tensor_tensor(rr[:, :, hf:], v[:, :, 0:hf], bc(sn[:, hf:], 1, 2 * HEADS),
                                        ALU.mult).then_inc(S["rope_parts"], 1)
                dve.wait_ge(S["rope_parts"], t + 1)
                nc.vector.tensor_tensor(qk[b][:], rc[:].rearrange("p h e -> p (h e)"), rr[:].rearrange("p h e -> p (h e)"),
                                        ALU.add).then_inc(S["rope_ready"], 1)

            def attention(g, behind, ahead):
                q = g + (GROUPS - 1)
                for j in range(GT):
                    t = GT * g + j
                    b = j % 2
                    dve.wait_ge(S["qkT_ready"], t + 1 + AHEAD)
                    nc.vector.tensor_tensor(qx[:], bc(qkT[b][:, 0:P], 1, HB), bc(head_mask, 2, P),
                                            ALU.mult).then_inc(S["qx_ready"], 1)
                    for h in range(4):
                        dve.wait_ge(S["score_out"], 4 * t + h + 1)
                        nc.vector.tensor_tensor(pr[:, h, :].rearrange("p (h t) -> p h t", h=HB),
                                                bank[4 + h % 2][:].rearrange("p (h t) -> p h t", h=HB),
                                                bc(tri, 1, HB), ALU.mult).then_inc(S["masked"], 1)
                    if j + 1 < GT:
                        bias_rope(g, j + 1)
                    dve.wait_ge(S["kv_out"], t + 1)
                    nc.vector.tensor_tensor(kvm[:], bank[2][:, 0:D], block_mask, ALU.mult).then_inc(S["kv_masked"], 1)
                    dve.wait_ge(S["kv_masked"], t + 1 + AHEAD)
                    dve.wait_ge(S["state_read"], t + 1)
                    nc.vector.tensor_tensor(state[:], state[:], kvm[:], ALU.add).then_inc(S["state_ready"], 1)
                    if behind:
                        if j == 0:
                            norm_f(q, g - 1)
                        if j == 1:
                            route_experts(q)
                        if j == 2:
                            route_counts(q)
                            shared_hidden(q, 0)
                    if ahead:
                        if j == 2:
                            combine(0, g + 1)
                        if j == 3:
                            norm_a(g + 1)
                    dve.wait_ge(S["attn_out"], t + 1)
                    xj = xres[:, bass.ds(t * D, D)]
                    nc.vector.tensor_tensor(xj, xj, bank[3][:, 0:D], ALU.add).then_inc(S["x2_ready"], 1)
                if ahead:
                    bias_rope(g + 1, 0)
                if behind:
                    shared_hidden(q, 1)
                    route_slots(q, g - 1)
                    shared_out(q, g - 1)

            def norm_a(g):
                dve.wait_ge(S["x1_ready"], g + 1)
                dve.wait_ge(S["xf_turned_a"], g + AHEAD)
                dve.sem_inc(passed["dve"], 1)
                norm("a", g, g)

            for name in ("shared_hidden", "qkv_biased", "kv_masked", "masked", "x2_ready", "state_ready", "seen_ready"):
                dve.sem_inc(S[name], AHEAD)
            nc.vector.memset(empty[:], 0.0).then_inc(S["empty_set"], 1)
            nc.vector.memset(zeros[:], 0.0).then_inc(S["empty_set"], 1)
            nc.vector.memset(seen[:], 0.0).then_inc(S["empty_set"], 1)
            nc.vector.memset(state[:], 0.0).then_inc(S["empty_set"], 1)
            nc.vector.memset(cenT[:], 0.0).then_inc(S["empty_set"], 1)
            for b in range(2):
                nc.vector.memset(vp[b][:], 0.0).then_inc(S["empty_set"], 1)
            dve.wait_ge(S["empty_set"], 7)
            nc.vector.memset(empty[:].bitcast(U32).rearrange("p (n r) -> p n r", r=ROW)[:, :, D + 1], FAR).then_inc(S["empty_set"], 1)
            dve.wait_ge(S["cen_in"], 16)
            nc.vector.tensor_tensor_reduce(cen_sq[:], cen[:], cen[:], 1.0, 0.0, ALU.mult, ALU.add,
                                           cen_n[:, 0:1]).then_inc(S["cen_square"], 1)
            dve.wait_ge(S["cen_root"], 1)
            nc.vector.tensor_scalar(cen_n[:, 2:3], cen_n[:, 1:2], 1e-12, None, ALU.max).then_inc(S["cen_inv0"], 1)
            dve.wait_ge(S["cen_inv0"], 1)
            nc.vector.reciprocal(cen_n[:, 3:4], cen_n[:, 2:3]).then_inc(S["cen_inv"], 1)
            dve.wait_ge(S["cen_inv"], 1)
            nc.vector.tensor_scalar(cen_sq[:], cen[:], cen_n[:, 3:4], None, ALU.mult).then_inc(S["cen_scaled"], 1)
            dve.wait_ge(S["cen_turned"], 1)
            nc.vector.tensor_copy(cenT[:, 0:NG + E], bank[2][:, 0:NG + E]).then_inc(S["cenT_ready"], 1)
            dve.wait_ge(S["consts_in"], 32)
            dve.wait_ge(S["small_in"], 16 * 5)
            dve.wait_ge(S["x_in"], 16)

            with dve.Fori(0, GROUPS) as g:
                feed_forward(g, g)
            experts(0)
            dve.wait_ge(S["seen_ready"], (GT + 1) * GROUPS + AHEAD)
            nc.vector.memset(seen[:, 0, :], 0.0).then_inc(S["empty_set"], 1)
            dve.wait_ge(S["empty_set"], 9)
            combine(0, 0)
            norm_a(0)
            bias_rope(0, 0)
            attention(0, False, True)
            with dve.Fori(1, GROUPS - 1) as g:
                attention(g, True, True)
            attention(GROUPS - 1, True, False)
            dve.wait_ge(S["x2_ready"], TILES + AHEAD)
            feed_forward(2 * GROUPS - 1, GROUPS - 1)
            experts(1)
            with dve.Fori(0, GROUPS) as g:
                combine(1, g)

        @block.scalar
        def _(act):
            def roots(kind, n):
                act.wait_ge(S[f"sq_ready_{kind}"], n + 1)
                nc.scalar.activation(rs[kind][:], sq[kind][:], ACT.Sqrt).then_inc(S[f"roots_{kind}"], 1)

            def turn_f(q):
                act.wait_ge(S["xf_turned_f"], q + 1 + AHEAD)
                act.wait_ge(S["gates_up"], HC * q + AHEAD)
                nc.scalar.activation(xfT["f"][:], bank[0][:], ACT.Copy).then_inc(S["xfT_ready_f"], 1)

            def turn_a(g):
                act.wait_ge(S["xf_turned_a"], g + 1 + AHEAD)
                act.wait_ge(S["qkv_out"], GT * g + AHEAD)
                nc.scalar.activation(xfT["a"][:], bank[0][:], ACT.Copy).then_inc(S["xfT_ready_a"], 1)

            def shared_gate(q, c):
                act.wait_ge(S["gates_up"], HC * q + c + 1 + AHEAD)
                act.wait_ge(S["shared_hidden"], HC * q + AHEAD)
                nc.scalar.activation(gs[:, c, :], bank[6][:], ACT.Silu).then_inc(S["shared_gate"], 1)

            def fill_rows(q):
                act.wait_ge(S["delta"], q + 1)
                nc.scalar.activation(th[:], dlt[:], ACT.Tanh, scale=0.5).then_inc(S["tanh_ready"], 1)
                act.wait_ge(S["rows_free"], q + AHEAD)
                for j in range(GT):
                    i = nc.scalar.activation(rows[:, j, :, 0:D], bc(xf["f"][:, j, :], 1, K), ACT.Copy)
                i.then_inc(S["rows_x"], 1)

            def feed_forward(q):
                roots("f", q)
                turn_f(q)
                shared_gate(q, 0)
                shared_gate(q, 1)
                fill_rows(q)

            def spread_values(g, j):
                act.wait_ge(S["qkv_biased"], GT * g + j + 1 + AHEAD)
                b = j % 2
                nc.scalar.activation(vp[b][:].rearrange("p (h x) -> p h x", h=HEADS)[:, :, 0:DH],
                                     qkv[b][:, 2 * D:].rearrange("p (h e) -> p h e", h=HEADS),
                                     ACT.Copy).then_inc(S["vp_ready"], 1)

            def attention(g, behind, ahead):
                q = g + (GROUPS - 1)
                for j in range(GT):
                    t = GT * g + j
                    act.wait_ge(S["qk_turned"], t + 1)
                    nc.scalar.activation(qkT[j % 2][:], bank[2][:, 0:2 * P], ACT.Copy).then_inc(S["qkT_ready"], 1)
                    spread_values(g, j)
                    if behind:
                        if j == 0:
                            roots("f", q)
                        if j >= 2:
                            shared_gate(q, j - 2)
                    if ahead and j == 3:
                        roots("a", g + 1)
                    act.wait_ge(S["oT_out"], t + 1)
                    nc.scalar.activation(oT[:], bank[3][:, 0:P], ACT.Copy).then_inc(S["oT_ready"], 1)
                    if behind and j == 0:
                        turn_f(q)
                    if ahead and j == 3:
                        turn_a(g + 1)
                if behind:
                    fill_rows(q)

            def turn_x(f, i, d):
                e = expert(f, i, d)
                act.wait_ge(S["x_turned"], e + 1)
                act.wait_ge(S["e_up_out"], e - 1 if d else E * f)
                nc.scalar.activation(xbT[d % 2][:], bank[0][:, 0:CAP], ACT.Copy).then_inc(S["xT_ready"], 1)

            def gate(f, i, d):
                e = expert(f, i, d)
                act.wait_ge(S["e_gate_out"], e + 1)
                act.wait_ge(S["e_hidden"], e)
                for c in range(HC):
                    a = nc.scalar.activation(eg[:, c, :], bank[1 + c][:, 0:CAP], ACT.Silu)
                a.then_inc(S["e_gate_act"], 1)

            def scale(f, i, d):
                e = expert(f, i, d)
                act.wait_ge(S["e_down"], e + 1)
                act.wait_ge(S["results_free"], e + AHEAD)
                for t, m in enumerate(SIZES):
                    a = nc.scalar.activation(eo[d % 2][0:m, t, :], bank[5 + d % 2][0:m, t * D:(t + 1) * D], ACT.Copy,
                                             scale=xb[d % XB][0:m, t, D:D + 1])
                a.then_inc(S["e_scaled"], 1)

            def experts(f):
                turn_x(f, 0, 0)
                turn_x(f, 0, 1)
                gate(f, 0, 0)

                def step(i, d):
                    if not (isinstance(i, int) and XB * i + d + 1 >= E):
                        turn_x(f, i, d + 1)
                    gate(f, i, d)
                    scale(f, i, d - 1)
                with act.Fori(0, E // XB - 1) as i:
                    for d in range(1, XB + 1):
                        step(i, d)
                for d in range(1, XB):
                    step(E // XB - 1, d)
                scale(f, E // XB - 1, XB - 1)

            for name in ("xfT_ready_a", "xfT_ready_f", "qkT_ready", "e_scaled", "rows_x"):
                act.sem_inc(S[name], AHEAD)
            act.wait_ge(S["cen_square"], 1)
            nc.scalar.activation(cen_n[:, 1:2], cen_n[:, 0:1], ACT.Sqrt).then_inc(S["cen_root"], 1)
            with act.Fori(0, GROUPS) as g:
                feed_forward(g)
            experts(0)
            roots("a", 0)
            turn_a(0)
            attention(0, False, True)
            with act.Fori(1, GROUPS - 1) as g:
                attention(g, True, True)
            attention(GROUPS - 1, True, False)
            feed_forward(2 * GROUPS - 1)
            experts(1)

        @block.tensor
        def _(pe):
            def turn(kind, n):
                for j in range(GT):
                    pe.wait_ge(S[f"xf_ready_{kind}"], GT * n + j + 1)
                    i = nc.tensor.transpose(bank[0][:, j * P:(j + 1) * P], xf[kind][:, j, :], ident)
                i.then_inc(S[f"xf_turned_{kind}"], 1)

            def router(q):
                pe.wait_ge(S["xfT_ready_f"], q + 1 + AHEAD)
                for j in range(GT):
                    i = nc.tensor.matmul(bank[6][:, j * P:(j + 1) * P], xfT["f"][:, j * P:(j + 1) * P], cenT[:],
                                         start=True, stop=True)
                i.then_inc(S["router_out"], 1)

            def gate_up_shared(q, c):
                if c == 0:
                    pe.wait_ge(S["scores_n"], q + 1)
                else:
                    pe.wait_ge(S["shared_hidden"], HC * q + c + AHEAD)
                nc.tensor.matmul(bank[6][:], w_sgu[:, c * P:(c + 1) * P], xfT["f"][:], start=True, stop=True)
                nc.tensor.matmul(bank[7][:], w_sgu[:, H + c * P:H + (c + 1) * P], xfT["f"][:], start=True,
                                 stop=True).then_inc(S["gates_up"], 1)

            def prefix(q):
                pe.wait_ge(S["seen_ready"], (GT + 1) * q + GT + AHEAD)
                pe.wait_ge(S["shared_gate"], HC * (q + 1))
                nc.tensor.matmul(bank[6][:, 0:GT * E], strict, cnt[:].rearrange("p j e -> p (j e)"), start=True, stop=False)
                nc.tensor.matmul(bank[6][:, 0:GT * E], ones, seen[:, 0:GT, :].rearrange("p j e -> p (j e)"),
                                 start=False, stop=True).then_inc(S["prefix_out"], 1)

            def down_shared(q):
                pe.wait_ge(S["shared_hidden"], HC * (q + 1) + AHEAD)
                for j in range(GT):
                    for c in range(HC):
                        i = nc.tensor.matmul(bank[7][:, j * D:(j + 1) * D], hs[:, c, j * P:(j + 1) * P],
                                             w_sd[:, c * D:(c + 1) * D], start=(c == 0), stop=(c == HC - 1))
                i.then_inc(S["shared_out"], 1)

            def feed_forward(q):
                turn("f", q)
                router(q)
                gate_up_shared(q, 0)
                gate_up_shared(q, 1)
                prefix(q)
                down_shared(q)

            def turn_x(f, i, d):
                e = expert(f, i, d)
                pe.wait_ge(s_xb[d % XB], (i + (E // XB * f + d // XB + 1)) * 32)
                pe.wait_ge(S["xT_ready"], e)
                for t, m in enumerate(SIZES):
                    a = nc.tensor.transpose(bank[0][:, t * P:t * P + m], xb[d % XB][0:m, t, 0:D], ident[0:m, 0:m])
                a.then_inc(S["x_turned"], 1)

            def gate_up(f, i, d):
                e = expert(f, i, d)
                w = w_e[d % WB]
                pe.wait_ge(s_w[d % WB], (i * (XB // WB) + (E // WB * f + d // WB + 1)) * 16)
                pe.wait_ge(S["xT_ready"], e + 1)
                pe.wait_ge(S["e_gate_act"], e)
                for c in range(2 * HC):
                    if c == HC:
                        pe.wait_ge(S["e_hidden"], e)
                    a = nc.tensor.matmul(bank[1 + c][:, 0:CAP], w[:, c * P:(c + 1) * P], xbT[d % 2][:], start=True, stop=True)
                    if c == HC - 1:
                        a.then_inc(S["e_gate_out"], 1)
                a.then_inc(S["e_up_out"], 1)

            def down(f, i, d):
                e = expert(f, i, d)
                pe.wait_ge(S["e_hidden"], e + 1)
                pe.wait_ge(S["e_scaled"], e + AHEAD)
                for t, m in enumerate(SIZES):
                    for c in range(HC):
                        a = nc.tensor.matmul(bank[5 + d % 2][0:m, t * D:(t + 1) * D], eh[d % 2][:, c, t * P:t * P + m],
                                             w_e[d % WB][:, 2 * H + c * D:2 * H + (c + 1) * D],
                                             start=(c == 0), stop=(c == HC - 1))
                a.then_inc(S["e_down"], 1)

            def experts(f):
                turn_x(f, 0, 0)
                turn_x(f, 0, 1)
                gate_up(f, 0, 0)

                def step(i, d):
                    if not (isinstance(i, int) and XB * i + d + 1 >= E):
                        turn_x(f, i, d + 1)
                    gate_up(f, i, d)
                    down(f, i, d - 1)
                with pe.Fori(0, E // XB - 1) as i:
                    for d in range(1, XB + 1):
                        step(i, d)
                for d in range(1, XB):
                    step(E // XB - 1, d)
                down(f, E // XB - 1, XB - 1)

            def project(g, j):
                pe.wait_ge(S["xfT_ready_a"], g + 1 + AHEAD)
                pe.wait_ge(S["qkv_biased"], GT * g + j + AHEAD)
                nc.tensor.matmul(bank[1][:, 0:3 * D], xfT["a"][:, j * P:(j + 1) * P], w_qkv[:], start=True,
                                 stop=True).then_inc(S["qkv_out"], 1)

            def attention(g, behind, ahead):
                q = g + (GROUPS - 1)
                for j in range(GT):
                    t = GT * g + j
                    b = j % 2
                    pe.wait_ge(S["rope_ready"], t + 1)
                    pe.wait_ge(S["kv_masked"], t + AHEAD)
                    nc.tensor.transpose(bank[2][:, 0:P], qk[b][:, 0:D], ident)
                    nc.tensor.transpose(bank[2][:, P:2 * P], qk[b][:, D:], ident).then_inc(S["qk_turned"], 1)
                    if j + 1 < GT:
                        project(g, j + 1)
                    pe.wait_ge(S["qkT_ready"], t + 1 + AHEAD)
                    nc.tensor.matmul(bank[2][:, 0:D], qk[b][:, D:], qkv[b][:, 2 * D:], start=True,
                                     stop=True).then_inc(S["kv_out"], 1)
                    pe.wait_ge(S["qx_ready"], t + 1)
                    for h in range(4):
                        pe.wait_ge(S["masked"], 4 * t + max(h - 1, 0) + AHEAD)
                        nc.tensor.matmul(bank[4 + h % 2][:], qkT[b][32 * h:32 * h + 32, P:2 * P],
                                         qx[32 * h:32 * h + 32, :, :].rearrange("p h t -> p (h t)"), start=True,
                                         stop=True).then_inc(S["score_out"], 1)
                    if behind:
                        if j == 1:
                            router(q)
                        if j >= 2:
                            gate_up_shared(q, j - 2)
                    pe.wait_ge(S["x2_ready"], t + AHEAD)
                    pe.wait_ge(S["state_ready"], t + AHEAD)
                    nc.tensor.matmul(bank[3][:, 0:P], state[:], qkT[b][:, 0:P], start=True,
                                     stop=False).then_inc(S["state_read"], 1)
                    pe.wait_ge(S["vp_ready"], t + 1)
                    for h in range(HEADS):
                        if h % HB == 0:
                            pe.wait_ge(S["masked"], 4 * t + h // HB + 1 + AHEAD)
                        i = nc.tensor.matmul(bank[3][:, 0:P], vp[b][:, h * D:(h + 1) * D],
                                             pr[:, h // HB, (h % HB) * P:(h % HB + 1) * P],
                                             start=False, stop=(h == HEADS - 1))
                    i.then_inc(S["oT_out"], 1)
                    if behind and j == 0:
                        pe.wait_ge(S["xfT_ready_a"], g + 1 + AHEAD)
                        turn("f", q)
                    if ahead and j == 3:
                        if behind:
                            pe.wait_ge(S["xfT_ready_f"], q + 1 + AHEAD)
                        turn("a", g + 1)
                    pe.wait_ge(S["oT_ready"], t + 1)
                    nc.tensor.transpose(bank[3][:, 0:P], oT[:], ident).then_inc(S["attn_out"], 1)
                if ahead:
                    project(g + 1, 0)
                if behind:
                    prefix(q)
                    down_shared(q)

            for name in ("xf_turned_a", "xf_turned_f", "gates_up", "qkv_out"):
                pe.sem_inc(S[name], AHEAD)
            pe.wait_ge(S["consts_in"], 32)
            pe.wait_ge(S["empty_set"], 8)
            pe.wait_ge(S["cen_scaled"], 1)
            nc.tensor.transpose(bank[2][:, 0:NG + E], cen_sq[:], ident[0:NG + E, 0:NG + E]).then_inc(S["cen_turned"], 1)
            pe.wait_ge(S["cenT_ready"], 1)
            pe.wait_ge(S["small_in"], 16 * 5)
            with pe.Fori(0, GROUPS) as g:
                feed_forward(g)
            pe.wait_ge(S["base_ready"], GROUPS)
            experts(0)
            pe.wait_ge(S["e_scaled"], E + AHEAD)
            turn("a", 0)
            project(0, 0)
            attention(0, False, True)
            with pe.Fori(1, GROUPS - 1) as g:
                attention(g, True, True)
            attention(GROUPS - 1, True, False)
            feed_forward(2 * GROUPS - 1)
            pe.wait_ge(S["base_ready"], 2 * GROUPS)
            experts(1)

        @block.gpsimd
        def _(pool):
            def dispatch(f, q):
                pool.wait_ge(S["rows_gate"], q + 1)
                pool.wait_ge(S["rows_x"], q + 1 + AHEAD)
                pool.sem_inc(passed["pool"], 1)
                for j in range(GT):
                    for k in range(K):
                        pool.indirect_dma_start(
                            slots[f], bass.IndirectOffsetOnAxis(ap=slot[:, j * K + k:j * K + k + 1], axis=0),
                            rows[:, j, k, :], None, bounds_check=last_slot, oob_is_err=False).then_inc(S["slots_sent"], 16)
                pool.wait_ge(S["slots_sent"], (q + 1) * (16 * GT * K))
                pool.sem_inc(S["rows_free"], 1)

            def results(f, i, d):
                pool.wait_ge(S["e_scaled"], expert(f, i, d) + 1 + AHEAD)
                pool.sem_inc(passed["pool"], 1)
                for t, m in enumerate(SIZES):
                    pool.indirect_dma_start(
                        routed[f], bass.IndirectOffsetOnAxis(ap=xb[d][:].bitcast(U32)[0:m, t, D + 1:D + 2], axis=0),
                        eo[d % 2][0:m, t, :], None, bounds_check=last_place, oob_is_err=False).then_inc(s_sc[d], 16)
                if not (f == 0 and isinstance(i, int) and d == 0):
                    pool.wait_ge(s_sc[(d - 1) % XB], sent_count(f, i, d - 1))
                    pool.sem_inc(S["results_free"], 1)

            for name in ("rows_free", "results_free"):
                pool.sem_inc(S[name], AHEAD * (2 if name == "results_free" else 1))
            last_slot = pool.to_reg(SLOTS - 1)
            last_place = pool.to_reg(TOKENS * K - 1)
            pool.wait_ge(S["empty_sent0"], 16 * 8)
            with pool.Fori(0, GROUPS) as g:
                dispatch(0, g)
            pool.wait_ge(S["zeros_sent0"], 16 * 8)
            for d in range(XB):
                results(0, 0, d)
            with pool.Fori(1, E // XB) as i:
                for d in range(XB):
                    results(0, i, d)
            pool.wait_ge(S["empty_sent1"], 16 * 8)
            with pool.Fori(0, GROUPS) as g:
                dispatch(1, GROUPS + g)
            pool.wait_ge(S["zeros_sent1"], 16 * 8)
            for d in range(XB):
                results(1, 0, d)
            with pool.Fori(1, E // XB) as i:
                for d in range(XB):
                    results(1, i, d)

        @block.sync
        def _(sp):
            def load_weights(b, e):
                sp.dma_start(w_e[b][:], ew[bass.ds(e, 1), :, :].rearrange("e p n -> (e p) n")).then_inc(s_w[b], 16)

            def load_slots(f, b, e):
                src = slots[f]
                sp.dma_start(xb[b][:, 0:FULL, :], src[bass.ds(e * CAP, FULL * P), :].rearrange("(t p) r -> p t r", p=P)
                             ).then_inc(s_xb[b], 16)
                sp.dma_start(xb[b][0:REST, FULL, :], src[bass.ds(e * CAP + FULL * P, REST), :]).then_inc(s_xb[b], 16)

            def fill_slots(f, c):
                a = slots[f].rearrange("(p n) r -> p (n r)", n=10)
                sp.dma_start(a[bass.ds(c * P, P), :], empty[:]).then_inc(S[f"empty_sent{f}"], 16)

            def fill_routed(f, c):
                z = routed[f].rearrange("(p n) d -> p (n d)", n=8)
                sp.dma_start(z[bass.ds(c * P, P), :], zeros[:]).then_inc(S[f"zeros_sent{f}"], 16)

            sp.dma_start(cen[:], cents).then_inc(S["cen_in"], 16)
            sp.dma_start(cst[:], consts).then_inc(S["consts_in"], 16)
            sp.dma_start(plc[:], places).then_inc(S["consts_in"], 16)
            sp.dma_start(xres[:].rearrange("p (t d) -> p t d", t=TILES), x_t).then_inc(S["x_in"], 16)
            sp.dma_start(w_sgu[:], sgu).then_inc(S["small_in"], 16)
            sp.dma_start(w_sd[:].rearrange("p (c d) -> p c d", c=HC), sd.rearrange("(c p) d -> p c d", p=P)).then_inc(S["small_in"], 16)
            sp.dma_start(w_qkv[:], wqkv).then_inc(S["small_in"], 16)
            sp.dma_start(b_qkv[:], bqkv.to_broadcast([P, 3 * D])).then_inc(S["small_in"], 16)
            sp.dma_start(e_bias[:], ebias.to_broadcast([P, E])).then_inc(S["small_in"], 16)
            sp.wait_ge(S["empty_set"], 8)
            for c in range(FILLS):
                fill_slots(0, c)
            for f in range(2):
                if f == 0:
                    sp.wait_ge(S["slot_ready"], 2)
                    for c in range(FILLS):
                        fill_routed(0, c)
                for d in range(WB):
                    load_weights(d, d)
                sp.wait_ge(S["slots_sent"], 16 * K * TILES * (f + 1))
                for d in range(XB):
                    load_slots(f, d, d)
                if f == 0:
                    for c in range(2):
                        fill_slots(1, c)
                        fill_routed(1, c)

                with sp.Fori(0, E // XB - 1) as i:
                    for d in range(XB):
                        sp.wait_ge(S["e_down"], expert(f, i, d) + 1)
                        sp.sem_inc(passed["sp"], 1)
                        load_weights(d % WB, expert(0, i, d) + WB)
                        sp.wait_ge(s_sc[d], sent_count(f, i, d))
                        sp.sem_inc(passed["sp"], 1)
                        load_slots(f, d, expert(0, i, d) + XB)
                        if f == 0 and d % (XB // 2) == 0:
                            c = 2 * i + (2 + d // (XB // 2))
                            fill_slots(1, c)
                            fill_routed(1, c)
                for d in range(XB - WB):
                    sp.wait_ge(S["e_down"], E * f + E - XB + d + 1)
                    load_weights(d % WB, E - WB + d)
                for d in range(XB):
                    sp.wait_ge(s_sc[d], 16 * ST * (E // XB) * (f + 1))
                with sp.Fori(0, GROUPS) as g:
                    sp.dma_start(yk[:, bass.ds(g * (GW * K), GW * K)].rearrange("p (j x) -> p j x", j=GT),
                                 routed[f][bass.ds(g * (GW * K), GW * K), :].rearrange("(j p k) d -> p j (k d)", p=P, k=K)
                                 ).then_inc(S["yk_in"], 16)
                    sp.wait_ge(S["yk_in"], 16 * (g + (GROUPS * f + 1)))
                    sp.sem_inc(passed["sp"], 1)
                if f:
                    with sp.Fori(0, GROUPS) as g:
                        sp.wait_ge(S["x1_ready"], g + (GROUPS + 1))
                        sp.sem_inc(passed["sp"], 1)
                        sp.dma_start(out_t[:, bass.ds(g * GT, GT), :], xres_of(g)).then_inc(S["out_sent"], 16)
            sp.wait_ge(S["out_sent"], 16 * GROUPS)


def kernel(L0_attn_x, L0_attn_W_qkv, L0_attn_b_qkv, L0_ffn_group_centroids, L0_ffn_expert_centroids, L0_ffn_bias,
           L0_ffn_wg, L0_ffn_wu, L0_ffn_wd, L0_ffn_sg, L0_ffn_su, L0_ffn_sd):
    import concourse.bacc as bacc
    from concourse.bass_utils import run_bass_kernel_spmd

    n = np.asarray
    consts, places = shape_constants()
    wd = n(L0_ffn_wd).reshape(E, HC, P, D).transpose(0, 2, 1, 3).reshape(E, P, HC * D)
    ins = {
        "x": n(L0_attn_x).reshape(TOKENS, D),
        "consts": consts,
        "places": places,
        "wqkv": n(L0_attn_W_qkv).T,
        "bqkv": n(L0_attn_b_qkv).reshape(1, 3 * D),
        "cents": np.concatenate([n(L0_ffn_group_centroids), n(L0_ffn_expert_centroids)], 0),
        "ebias": n(L0_ffn_bias).reshape(1, E),
        "ew": np.concatenate([n(L0_ffn_wg), n(L0_ffn_wu), wd], 2),
        "sgu": np.concatenate([n(L0_ffn_sg), n(L0_ffn_su)], 1),
        "sd": n(L0_ffn_sd),
    }
    ins = {k: np.ascontiguousarray(v) for k, v in ins.items()}
    nc = bacc.Bacc("TRN2", target_bir_lowering=False, num_devices=1)
    args = {k: nc.dram_tensor(k, v.shape, mybir.dt.from_np(v.dtype), kind="ExternalInput").ap() for k, v in ins.items()}
    args["out"] = nc.dram_tensor("out", (TOKENS, D), F32, kind="ExternalOutput").ap()
    macaron(nc, **args)
    r = run_bass_kernel_spmd(nc, [ins], core_ids=[0])
    return r.results[0]["out"].reshape(1, TOKENS, D)
```

```python
from contextlib import ExitStack

import numpy as np

import concourse.bass as bass
from concourse import mybir

F32 = mybir.dt.float32
U32 = mybir.dt.uint32
ALU = mybir.AluOpType
ACT = mybir.ActivationFunctionType
AX = mybir.AxisListType

P = 128
D = 128
TOKENS = 2048
TILES = TOKENS // P
GT = 4
GROUPS = TILES // GT
GW = GT * P
E = 32
NG = 8
EPG = E // NG
K = 4
H = 256
HC = H // P
CAP = max(1, int(TOKENS / E * K * 1.25))
FULL = CAP // P
REST = CAP - FULL * P
ST = FULL + 1
SLOTS = E * CAP
FAR = 1 << 16
ROW = D + 2
HEADS = 16
DH = D // HEADS
HB = 4
ROPE_BASE = 10000.0
LN_EPS = 1e-5
SIZES = [P] * FULL + [REST]
FILLS = 8
XB = 8
RB = 4
KEPT0 = 4

C_IDENT, C_TRI, C_STRICT, C_ONES, C_BLOCK = (i * P for i in range(5))
C_HEAD = 5 * P
C_IOTA = C_HEAD + HB
C_COS = C_IOTA + E
C_SIN = C_COS + TILES * DH
C_ALL = C_SIN + TILES * DH


def shape_constants():
    c = np.zeros((P, C_ALL), np.float32)
    i = np.arange(P)
    c[:, C_IDENT:C_IDENT + P] = i[:, None] == i[None, :]
    c[:, C_TRI:C_TRI + P] = i[:, None] <= i[None, :]
    c[:, C_STRICT:C_STRICT + P] = i[:, None] < i[None, :]
    c[:, C_ONES:C_ONES + P] = 1.0
    c[:, C_BLOCK:C_BLOCK + P] = i[:, None] // DH == i[None, :] // DH
    c[:, C_HEAD:C_HEAD + HB] = (i[:, None] // DH) % HB == np.arange(HB)[None, :]
    c[:, C_IOTA:C_IOTA + E] = np.arange(E)[None, :]
    freq = np.float32(1) / np.float32(ROPE_BASE) ** (np.arange(0, DH, 2, dtype=np.float32) / np.float32(DH))
    ang = np.arange(TOKENS, dtype=np.float32)[:, None] * freq[None, :]
    cos = np.concatenate([np.cos(ang), np.cos(ang)], 1)
    sin = np.concatenate([-np.sin(ang), np.sin(ang)], 1)
    for at, t in ((C_COS, cos), (C_SIN, sin)):
        c[:, at:at + TILES * DH] = t.reshape(TILES, P, DH).transpose(1, 0, 2).reshape(P, -1)
    place = (np.arange(TILES)[None, :, None] * P + i[:, None, None]) * K + np.arange(K)[None, None, :]
    return c, np.ascontiguousarray(place.reshape(P, TILES * K)).astype(np.uint32)


def macaron(nc, x, consts, places, wqkv, bqkv, cents, ebias, ew, sgu, sd, out):
    x_t = x.rearrange("(t p) d -> p t d", p=P)
    out_t = out.rearrange("(t p) d -> p t d", p=P)

    with ExitStack() as ctx:
        def sb(name, shape, dt=F32):
            return ctx.enter_context(nc.sbuf_tensor(name, shape, dt))

        def sem(name):
            return ctx.enter_context(nc.semaphore(name))

        slots = [nc.dram_tensor(f"slots{f}", [SLOTS, ROW], F32, kind="Internal").ap() for f in range(2)]
        routed = [nc.dram_tensor(f"routed{f}", [TOKENS * K, D], F32, kind="Internal").ap() for f in range(2)]

        bank = [ctx.enter_context(nc.psum_tensor(f"bank{i}", [P, 512], F32)) for i in range(8)]

        cst = sb("cst", [P, C_ALL])
        plc = sb("plc", [P, TILES * K], U32)
        w_qkv = sb("w_qkv", [P, 3 * D])
        b_qkv = sb("b_qkv", [P, 3 * D])
        cen = sb("cen", [NG + E, D])
        cen_sq = sb("cen_sq", [NG + E, D])
        cen_n = sb("cen_n", [NG + E, 4])
        cenT = sb("cenT", [P, P])
        e_bias = sb("e_bias", [P, E])
        w_sgu = sb("w_sgu", [P, 2 * H])
        w_sd = sb("w_sd", [P, HC * D])
        zeros = sb("zeros", [P, D])
        empty = sb("empty", [P, ROW])

        xres = sb("xres", [P, TILES * D])
        span = {"a": GT, "f": GT, "h": GT, "i": TILES - GT}
        st = {k: sb(f"st_{k}", [P, n, 6]) for k, n in span.items()}
        mv = {k: sb(f"mv_{k}", [P, n, 2]) for k, n in span.items()}
        ve = {k: sb(f"ve_{k}", [P, n]) for k, n in span.items()}
        sq = {k: sb(f"sq_{k}", [P, 2, n]) for k, n in span.items()}
        rs = {k: sb(f"rs_{k}", [P, 2, n]) for k, n in span.items()}
        xf = {k: sb(f"xf_{k}", [P, GT, D]) for k in "af"}
        xfT = {k: sb(f"xfT_{k}", [P, GW]) for k in "af"}
        rn0 = {k: sb(f"rn0_{k}", [P, span[k]]) for k in "fhi"}
        rn_first = sb("rn_first", [P, TILES])
        rn = {"f": sb("rn_f", [P, GT]), "h": rn_first[:, 0:GT], "i": rn_first[:, GT:]}

        gs = sb("gs", [P, HC, GW])
        hs = sb("hs", [P, HC, GW])
        sc = sb("sc", [P, GT, NG + E])
        es = sb("es", [P, GT, E])
        g8 = sb("g8", [P, GT, 8])
        gi8 = sb("gi8", [P, GT, 8], U32)
        gif = sb("gif", [P, GT, K])
        geq = sb("geq", [P, GT * K, NG])
        gm = sb("gm", [P, GT, NG])
        pen = sb("pen", [P, GT, NG])
        mk0 = sb("mk0", [P, GT * NG, EPG])
        mk = sb("mk", [P, GT * NG, EPG])
        v8 = sb("v8", [P, GT, 8])
        vi8 = sb("vi8", [P, GT, 8], U32)
        eif = sb("eif", [P, GT, K])
        dlt = sb("dlt", [P, GT, K])
        th = sb("th", [P, GT, K])
        num = sb("num", [P, GT, K])
        den = sb("den", [P, GT, K])
        rden = sb("rden", [P, GT, K])
        ex = sb("ex", [P, GT, K])
        sm = sb("sm", [P, GT])
        rsm = sb("rsm", [P, GT])
        oh = sb("oh", [P, GT * K, E])
        cnt = sb("cnt", [P, GT, E])
        seen = sb("seen", [P, GT + 1, E])
        pe_ = sb("pe_", [P, GT * K, E])
        pos = sb("pos", [P, GT * K])
        far = sb("far", [P, GT * K])
        slot0 = sb("slot0", [P, GT * K])
        slot = [sb(f"slot_index{b}", [P, GT * K], U32) for b in range(2)]
        rows0 = sb("rows0", [P, GT, K, ROW])

        kept = sb("kept", [P, 2, KEPT0 + E + XB], U32)
        w_e = [sb(f"w_e{b}", [P, 3 * H]) for b in range(XB)]
        slot_rows = sb("slot_rows", [P, XB * ST * ROW])
        xb = [slot_rows[:, b * ST * ROW:(b + 1) * ST * ROW].rearrange("p (t r) -> p t r", t=ST) for b in range(XB)]
        xbT = [sb(f"xbT{b}", [P, CAP]) for b in range(2)]
        eg = sb("eg", [P, HC, CAP])
        eh = [sb(f"eh{b}", [P, HC, CAP]) for b in range(2)]
        eo = [sb(f"eo{b}", [P, ST, D]) for b in range(RB)]

        yk = sb("yk", [P, GROUPS * GT * K * D])
        y2 = sb("y2", [P, GT, 2 * D])
        y1 = sb("y1", [P, GT, D])

        qkv = [sb(f"qkv{b}", [P, 3 * D]) for b in range(2)]
        rc = sb("rc", [P, 2 * HEADS, DH])
        rr = sb("rr", [P, 2 * HEADS, DH])
        qk = [sb(f"qk{b}", [P, 2 * D]) for b in range(2)]
        qkT = [sb(f"qkT{b}", [P, 2 * P]) for b in range(2)]
        qx = sb("qx", [P, HB, P])
        pr = [sb(f"pr{b}", [P, HB, 4 * P]) for b in range(2)]
        vp = [sb(f"vp{b}", [P, HEADS * (D + DH)]) for b in range(2)]
        oT = sb("oT", [P, P])
        kvm = sb("kvm", [P, D])
        state = sb("state", [P, D])

        ident = cst[:, C_IDENT:C_IDENT + P]
        tri = cst[:, C_TRI:C_TRI + P]
        strict = cst[:, C_STRICT:C_STRICT + P]
        ones = cst[:, C_ONES:C_ONES + P]
        block_mask = cst[:, C_BLOCK:C_BLOCK + P]
        head_mask = cst[:, C_HEAD:C_HEAD + HB]
        iota = cst[:, C_IOTA:C_IOTA + E]

        names = """consts_in small_in x_in first_x_in empty_set empty_sent0 zeros_sent0
            empty_sent1 zeros_sent1 cen_in cen_square cen_root cen_inv0 cen_inv cen_scaled cen_turned cenT_ready
            norm_steps_a sq_ready_a roots_a xf_ready_a xf_turned_a xfT_ready_a
            norm_steps_h sq_ready_h roots_h norm_floor_h norm_inv_h
            norm_steps_i sq_ready_i roots_i xf_ready_i xf_turned_i xfT_ready_i
            norm_floor_i norm_inv_i norm_floor_f norm_inv_f
            norm_steps_f sq_ready_f roots_f xf_ready_f xf_turned_f xfT_ready_f
            router_out gates_up vp_ready state_read oT_out oT_ready shared_gate shared_hidden shared_out base_ready
            scores_n es_ready g_top g_idx g_idxf g_eq g_mask g_pen mk_half mk_ready v_top v_idx v_idxf
            delta tanh_ready e_num e_den e_rden e_exp e_sum e_rsum hot count seen_ready prefix_out
            rows_free results_free pos_part pos_ready far_ready slot_half slot_ready rows_x rows_gate
            x_turned xT_ready e_gate_out e_up_out e_gate_act e_hidden e_down e_scaled
            y_pairs y_sum x1_ready qkv_out qkv_biased rope_parts rope_ready qk_turned qkT_ready
            qx_ready score_out masked attn_out kv_out x2_ready kv_masked state_ready out_sent totals_out kept_ready""".split()
        S = {n: sem(n) for n in names}
        passed = {e: sem(f"passed_{e}") for e in ("dve", "pool", "sp")}
        AHEAD = 1
        s_w = [sem(f"weights_in{b}") for b in range(XB)]
        s_xb = [sem(f"slots_in{b}") for b in range(XB)]
        s_rows = [sem(f"slots_sent{b}") for b in range(2)]
        s_yk = [sem(f"yk_in{g}") for g in range(GROUPS)]
        s_first = [sem(f"first_sent{b}") for b in range(RB)]
        s_others = [sem(f"others_sent{b}") for b in range(RB)]

        block = ctx.enter_context(nc.Block())

        def sent_before(kind, q):
            return q + (2 if kind == "f" else 1) * AHEAD

        def bc(ap, axis, n):
            shape = list(ap.shape)
            shape.insert(axis, n)
            return ap.unsqueeze(axis).to_broadcast(shape)

        def expert(f, i, d):
            return XB * i + (E * f + d)

        def normed(kind, g):
            return (yk[:, bass.ds(g * GW, GW)].rearrange("p (j d) -> p j d", j=GT) if kind in "hi" else xf[kind][:])

        def turned(kind, g):
            return yk[:, bass.ds(g * GW + TILES * D, GW)] if kind == "i" else xfT[kind][:]

        def rows_of(b):
            return (slot_rows[:, 0:GT * K * ROW].rearrange("p (j k r) -> p j k r", j=GT, k=K) if b else rows0[:])

        def gates_of(kind, c):
            return bank[2 + c if kind == "i" else 7]

        def ups_of(kind, c):
            return bank[4 + c if kind == "i" else 0]

        def out_of(kind):
            return bank[0 if kind == "i" else 7]

        def xres_of(g):
            return xres[:, bass.ds(g * GW, GW)].rearrange("p (j d) -> p j d", j=GT)

        def is_tile(g, j):
            return not isinstance(g, int) or 0 <= GT * g + j < TILES

        @block.vector
        def _(dve):
            def norm_stats(kind, n, g):
                tiles = span[kind]
                xr = xres[:, bass.ds(g * GW, tiles * D)].rearrange("p (j d) -> p j d", j=tiles)
                for j in range(tiles):
                    i = nc.vector.bn_stats(st[kind][:, j, :], xr[:, j, :])
                i.then_inc(S[f"norm_steps_{kind}"], 1)
                dve.wait_ge(S[f"norm_steps_{kind}"], 4 * n + 1)
                dve.sem_inc(passed["dve"], 1)
                for j in range(tiles):
                    i = nc.vector.bn_aggr(mv[kind][:, j, :], st[kind][:, j, :])
                i.then_inc(S[f"norm_steps_{kind}"], 1)
                dve.wait_ge(S[f"norm_steps_{kind}"], 4 * n + 2)
                nc.vector.tensor_scalar(ve[kind][:], mv[kind][:, :, 1], LN_EPS, None, ALU.add).then_inc(S[f"norm_steps_{kind}"], 1)
                dve.wait_ge(S[f"norm_steps_{kind}"], 4 * n + 3)
                nc.vector.reciprocal(sq[kind][:, 0, :], ve[kind][:]).then_inc(S[f"norm_steps_{kind}"], 1)
                dve.wait_ge(S[f"norm_steps_{kind}"], 4 * n + 4)
                nc.vector.scalar_tensor_tensor(out=sq[kind][:, 1, :], in0=mv[kind][:, :, 1], scalar=float(D),
                                               in1=sq[kind][:, 0, :], op0=ALU.mult,
                                               op1=ALU.mult).then_inc(S[f"sq_ready_{kind}"], 1)

            def norm_apply(kind, n, g, at=0):
                xr = xres_of(g)
                dve.wait_ge(S[f"roots_{kind}"], n + 1)
                for j in range(GT):
                    nc.vector.tensor_scalar(normed(kind, g)[:, j, :], xr[:, j, :], mv[kind][:, at + j, 0:1],
                                            rs[kind][:, 0, at + j:at + j + 1],
                                            ALU.subtract, ALU.mult).then_inc(S["xf_ready_" + ("i" if kind == "h" else kind)], 1)

            def norm_lengths(kind, n):
                nc.vector.tensor_scalar(rn0[kind][:], rs[kind][:, 1, :], 1e-12, None, ALU.max).then_inc(S[f"norm_floor_{kind}"], 1)
                dve.wait_ge(S[f"norm_floor_{kind}"], n + 1)
                nc.vector.reciprocal(rn[kind][:], rn0[kind][:]).then_inc(S[f"norm_inv_{kind}"], 1)

            def apply_f(q, g):
                dve.wait_ge(S["xf_turned_f"], q - GROUPS + AHEAD)
                dve.wait_ge(S["rows_x"], q + AHEAD)
                norm_apply("f", q - GROUPS, g)
                norm_lengths("f", q - GROUPS)

            def apply_a(g):
                dve.wait_ge(S["xf_turned_a"], g + AHEAD)
                norm_apply("a", g, g)

            def route_experts(kind, q, g):
                if kind == "f":
                    dve.wait_ge(S["norm_inv_f"], q - GROUPS + 1)
                    lengths = rn["f"][:]
                else:
                    lengths = rn_first[:, bass.ds(g * GT, GT)]
                dve.wait_ge(S["router_out"], q + 1)
                nc.vector.tensor_tensor(sc[:], bank[6][:].rearrange("p (j e) -> p j e", j=GT)[:, :, 0:NG + E],
                                        bc(lengths, 2, NG + E), ALU.mult).then_inc(S["scores_n"], 1)
                dve.wait_ge(S["scores_n"], q + 1)
                nc.vector.tensor_tensor(es[:], sc[:, :, NG:], bc(e_bias[:], 1, GT), ALU.add).then_inc(S["es_ready"], 1)
                for j in range(GT):
                    i = nc.vector.max(g8[:, j, :], sc[:, j, 0:NG])
                i.then_inc(S["g_top"], 1)
                dve.wait_ge(S["g_top"], q + 1)
                dve.sem_inc(passed["dve"], 1)
                for j in range(GT):
                    i = nc.vector.max_index(gi8[:, j, :], g8[:, j, :], sc[:, j, 0:NG])
                i.then_inc(S["g_idx"], 1)
                dve.wait_ge(S["g_idx"], q + 1)
                nc.vector.tensor_copy(gif[:], gi8[:, :, 0:K]).then_inc(S["g_idxf"], 1)
                dve.wait_ge(S["g_idxf"], q + 1)
                nc.vector.tensor_tensor(geq[:], bc(gif[:].rearrange("p j k -> p (j k)"), 2, NG),
                                        bc(iota[:, 0:NG], 1, GT * K), ALU.is_equal).then_inc(S["g_eq"], 1)
                dve.wait_ge(S["g_eq"], q + 1)
                nc.vector.tensor_reduce(gm[:], geq[:].rearrange("p (j k) g -> p j g k", k=K), AX.X,
                                        ALU.add).then_inc(S["g_mask"], 1)
                dve.wait_ge(S["g_mask"], q + 1)
                nc.vector.tensor_scalar(pen[:], gm[:], 1e9, -1e9, ALU.mult, ALU.add).then_inc(S["g_pen"], 1)
                dve.wait_ge(S["es_ready"], q + 1)
                nc.vector.tensor_tensor(mk0[:], es[:].rearrange("p j (g e) -> p (j g) e", e=EPG),
                                        bc(gm[:].rearrange("p j g -> p (j g)"), 2, EPG), ALU.mult).then_inc(S["mk_half"], 1)
                dve.wait_ge(S["mk_half"], q + 1)
                dve.wait_ge(S["g_pen"], q + 1)
                nc.vector.tensor_tensor(mk[:], mk0[:], bc(pen[:].rearrange("p j g -> p (j g)"), 2, EPG),
                                        ALU.add).then_inc(S["mk_ready"], 1)
                dve.wait_ge(S["mk_ready"], q + 1)
                dve.sem_inc(passed["dve"], 1)
                mkj = mk[:].rearrange("p (j g) e -> p j (g e)", j=GT)
                for j in range(GT):
                    i = nc.vector.max(v8[:, j, :], mkj[:, j, :])
                i.then_inc(S["v_top"], 1)
                dve.wait_ge(S["v_top"], q + 1)
                dve.sem_inc(passed["dve"], 1)
                for j in range(GT):
                    i = nc.vector.max_index(vi8[:, j, :], v8[:, j, :], mkj[:, j, :])
                i.then_inc(S["v_idx"], 1)
                nc.vector.tensor_tensor(dlt[:], v8[:, :, 0:K], v8[:, :, 0:1].to_broadcast([P, GT, K]),
                                        ALU.subtract).then_inc(S["delta"], 1)

            def route_counts(q):
                dve.wait_ge(S["v_idx"], q + 1)
                nc.vector.tensor_copy(eif[:], vi8[:, :, 0:K]).then_inc(S["v_idxf"], 1)
                dve.wait_ge(S["v_idxf"], q + 1)
                nc.vector.tensor_tensor(oh[:], bc(eif[:].rearrange("p j k -> p (j k)"), 2, E),
                                        bc(iota, 1, GT * K), ALU.is_equal).then_inc(S["hot"], 1)
                dve.wait_ge(S["hot"], q + 1)
                nc.vector.tensor_reduce(cnt[:], oh[:].rearrange("p (j k) e -> p j e k", k=K), AX.X,
                                        ALU.add).then_inc(S["count"], 1)
                dve.wait_ge(S["count"], q + 1)
                dve.wait_ge(S["seen_ready"], (GT + 1) * q + AHEAD)
                for j in range(GT):
                    nc.vector.tensor_tensor(seen[:, j + 1, :], seen[:, j, :], cnt[:, j, :],
                                            ALU.add).then_inc(S["seen_ready"], 1)
                    dve.wait_ge(S["seen_ready"], (GT + 1) * q + j + 1 + AHEAD)

            def shared_hidden(kind, q, c):
                dve.wait_ge(S["gates_up"], HC * q + c + 1 + AHEAD)
                dve.wait_ge(S["shared_gate"], HC * q + c + 1)
                nc.vector.tensor_tensor(hs[:, c, :], gs[:, c, :], ups_of(kind, c)[:], ALU.mult).then_inc(S["shared_hidden"], 1)

            def route_slots(kind, q, g, b):
                rows = rows_of(b)
                dve.wait_ge(S["tanh_ready"], q + 1)
                nc.vector.tensor_scalar(num[:], th[:], 1.0, None, ALU.add).then_inc(S["e_num"], 1)
                nc.vector.tensor_scalar(den[:], th[:], -1.0, 1.0, ALU.mult, ALU.add).then_inc(S["e_den"], 1)
                dve.wait_ge(S["e_den"], q + 1)
                nc.vector.reciprocal(rden[:], den[:]).then_inc(S["e_rden"], 1)
                dve.wait_ge(S["e_num"], q + 1)
                dve.wait_ge(S["e_rden"], q + 1)
                nc.vector.tensor_tensor(ex[:], num[:], rden[:], ALU.mult).then_inc(S["e_exp"], 1)
                dve.wait_ge(S["e_exp"], q + 1)
                nc.vector.tensor_reduce(sm[:], ex[:], AX.X, ALU.add).then_inc(S["e_sum"], 1)
                dve.wait_ge(S["e_sum"], q + 1)
                nc.vector.reciprocal(rsm[:], sm[:]).then_inc(S["e_rsum"], 1)
                dve.wait_ge(S["prefix_out"], q + 1)
                nc.vector.tensor_tensor(
                    pe_[:].rearrange("p (j k) e -> p j k e", k=K), oh[:].rearrange("p (j k) e -> p j k e", k=K),
                    bc(bank[6][:, 0:GT * E].rearrange("p (j e) -> p j e", j=GT), 2, K),
                    ALU.mult).then_inc(S["pos_part"], 1)
                dve.wait_ge(S["pos_part"], q + 1)
                nc.vector.tensor_copy(seen[:, 0, :], seen[:, GT, :]).then_inc(S["seen_ready"], 1)
                nc.vector.tensor_reduce(pos[:], pe_[:], AX.X, ALU.add).then_inc(S["pos_ready"], 1)
                dve.wait_ge(S["pos_ready"], q + 1)
                nc.vector.tensor_scalar(far[:], pos[:], float(CAP), float(FAR), ALU.is_ge, ALU.mult).then_inc(S["far_ready"], 1)
                nc.vector.scalar_tensor_tensor(out=slot0[:], in0=eif[:].rearrange("p j k -> p (j k)"), scalar=float(CAP),
                                               in1=pos[:], op0=ALU.mult, op1=ALU.add).then_inc(S["slot_half"], 1)
                dve.wait_ge(S["far_ready"], q + 1)
                dve.wait_ge(S["slot_half"], q + 1)
                if not (kind == "f" and b):
                    dve.wait_ge(S["rows_free"], sent_before(kind, q))
                nc.vector.tensor_tensor(slot[b][:], slot0[:], far[:], ALU.add).then_inc(S["slot_ready"], 1)
                dve.wait_ge(S["e_rsum"], q + 1)
                nc.vector.scalar_tensor_tensor(out=rows[:, :, :, D], in0=ex[:], scalar=0.5,
                                                   in1=rsm[:].unsqueeze(2).to_broadcast([P, GT, K]),
                                                   op0=ALU.mult, op1=ALU.mult)
                nc.vector.tensor_copy(rows.bitcast(U32)[:, :, :, D + 1],
                                      plc[:, bass.ds(g * (GT * K), GT * K)].rearrange("p (j k) -> p j k", j=GT)
                                      ).then_inc(S["rows_gate"], 1)

            def shared_out(kind, q, g):
                dve.wait_ge(S["shared_out"], q + 1)
                xr = xres_of(g)
                nc.vector.scalar_tensor_tensor(out=xr.rearrange("p j d -> p (j d)"), in0=out_of(kind)[:], scalar=0.5,
                                               in1=xr.rearrange("p j d -> p (j d)"), op0=ALU.mult,
                                               op1=ALU.add).then_inc(S["base_ready"], 1)

            def feed_forward(kind, q, g, b):
                route_experts(kind, q, g)
                route_counts(q)
                route_slots(kind, q, g, b)
                shared_hidden(kind, q, 0)
                shared_hidden(kind, q, 1)
                shared_out(kind, q, g)

            def hidden(f, i, b, width):
                e = E * f + 2 * i + b
                dve.wait_ge(S["e_gate_act"], e + 1)
                dve.wait_ge(S["e_up_out"], e + 1)
                for c in range(HC):
                    m = nc.vector.tensor_tensor(eh[b][:, c, 0:width], eg[:, c, 0:width], bank[3 + c][:, 0:width], ALU.mult)
                m.then_inc(S["e_hidden"], 1)

            def experts(f):
                dve.wait_ge(S["totals_out"], f + 1)
                nc.vector.tensor_copy(kept[0:1, f, KEPT0:KEPT0 + E], bank[6][0:1, 0:E]).then_inc(S["kept_ready"], 1)
                dve.wait_ge(S["kept_ready"], f + 1)
                with dve.Fori(0, E // 2) as i:
                    dve.reg_load(tokens, kept[0:1, f, bass.ds(2 * i + KEPT0, 2)])
                    for b in range(2):
                        with dve.If_lt(tokens[b], P + 1):
                            hidden(f, i, b, P)
                        with dve.Else():
                            with dve.If_lt(tokens[b], 2 * P + 1):
                                hidden(f, i, b, 2 * P)
                            with dve.Else():
                                hidden(f, i, b, CAP)

            def combine(f, g):
                n = GROUPS * f + g
                dve.wait_ge(s_yk[g], 16 * (f + 1))
                y = yk[:, g * GW * K:(g + 1) * GW * K].rearrange("p (j k) -> p j k", j=GT)
                nc.vector.tensor_tensor(y2[:], y[:, :, 0:2 * D], y[:, :, 2 * D:], ALU.add).then_inc(S["y_pairs"], 1)
                dve.wait_ge(S["y_pairs"], n + 1)
                nc.vector.tensor_tensor(y1[:], y2[:, :, 0:D], y2[:, :, D:], ALU.add).then_inc(S["y_sum"], 1)
                dve.wait_ge(S["y_sum"], n + 1)
                dve.wait_ge(S["base_ready"], GROUPS * (f + 1) + AHEAD)
                xr = xres_of(g)
                nc.vector.tensor_tensor(xr, xr, y1[:], ALU.add).then_inc(S["x1_ready"], 1)

            def bias_rope(g, j):
                t = GT * g + j
                b = j % 2
                dve.wait_ge(S["qkv_out"], t + 1 + AHEAD)
                if is_tile(g, j - 2):
                    dve.wait_ge(S["vp_ready"], t - 1)
                nc.vector.tensor_tensor(qkv[b][:], bank[1][:, 0:3 * D], b_qkv[:], ALU.add).then_inc(S["qkv_biased"], 1)
                dve.wait_ge(S["qkv_biased"], t + 1 + AHEAD)
                v = qkv[b][:, 0:2 * D].rearrange("p (h e) -> p h e", e=DH)
                cs = cst[:, bass.ds(t * DH + C_COS, DH)]
                sn = cst[:, bass.ds(t * DH + C_SIN, DH)]
                hf = DH // 2
                nc.vector.tensor_tensor(rc[:], v, bc(cs, 1, 2 * HEADS), ALU.mult)
                nc.vector.tensor_tensor(rr[:, :, 0:hf], v[:, :, hf:], bc(sn[:, 0:hf], 1, 2 * HEADS), ALU.mult)
                nc.vector.tensor_tensor(rr[:, :, hf:], v[:, :, 0:hf], bc(sn[:, hf:], 1, 2 * HEADS),
                                        ALU.mult).then_inc(S["rope_parts"], 1)
                dve.wait_ge(S["rope_parts"], t + 1)
                nc.vector.tensor_tensor(qk[b][:], rc[:].rearrange("p h e -> p (h e)"), rr[:].rearrange("p h e -> p (h e)"),
                                        ALU.add).then_inc(S["rope_ready"], 1)

            def mask(g, j, h):
                dve.wait_ge(S["score_out"], 4 * GT * g + (4 * j + h + 1))
                nc.vector.tensor_tensor(pr[j % 2][:, h, :].rearrange("p (h t) -> p h t", h=HB),
                                        bank[4 + h % 2][:].rearrange("p (h t) -> p h t", h=HB),
                                        bc(tri, 1, HB), ALU.mult).then_inc(S["masked"], 1)

            def keep_own(g, j):
                dve.wait_ge(S["state_ready"], GT * g + j + AHEAD)
                dve.wait_ge(S["kv_out"], GT * g + j + 1)
                nc.vector.tensor_tensor(kvm[:], bank[2][:, 0:D], block_mask, ALU.mult).then_inc(S["kv_masked"], 1)

            def add_state(g, j):
                t = GT * g + j
                dve.wait_ge(S["kv_masked"], t + 1 + AHEAD)
                dve.wait_ge(S["state_read"], t + 1)
                nc.vector.tensor_tensor(state[:], state[:], kvm[:], ALU.add).then_inc(S["state_ready"], 1)

            def add_attention(g, j):
                t = GT * g + j
                dve.wait_ge(S["attn_out"], t + 1)
                xj = xres[:, bass.ds(t * D, D)]
                nc.vector.tensor_tensor(xj, xj, bank[6][:, 0:D], ALU.add).then_inc(S["x2_ready"], 1)

            def attention(g, j, behind, ahead):
                q = g + (GROUPS - 1)
                if is_tile(g, j + 2):
                    bias_rope(g, j + 2)
                if is_tile(g, j):
                    add_state(g, j)
                if is_tile(g, j + 1):
                    mask(g, j + 1, 0)
                if is_tile(g, j - 1):
                    add_attention(g, j - 1)
                if is_tile(g, j + 1):
                    mask(g, j + 1, 1)
                    keep_own(g, j + 1)
                if j == 0:
                    if ahead:
                        dve.wait_ge(S["x1_ready"], g + 2)
                        dve.sem_inc(passed["dve"], 1)
                        norm_stats("a", g + 1, g + 1)
                    if behind:
                        dve.wait_ge(S["x2_ready"], GT * g + AHEAD)
                        dve.sem_inc(passed["dve"], 1)
                        norm_stats("f", q - GROUPS, g - 1)
                    if ahead:
                        apply_a(g + 1)
                    if behind:
                        apply_f(q, g - 1)
                if j in (1, 2) and not behind:
                    combine(0, j + 1)
                if j == 1 and behind:
                    route_experts("f", q, g - 1)
                if j == 2 and behind:
                    route_counts(q)
                if j == 3 and behind:
                    route_slots("f", q, g - 1, 0)
                    shared_hidden("f", q, 1)
                if is_tile(g, j + 1):
                    mask(g, j + 1, 2)
                    mask(g, j + 1, 3)
                if j == 2 and behind:
                    shared_hidden("f", q, 0)
                if j == 3 and behind:
                    shared_out("f", q, g - 1)

            tokens = [dve.alloc_register(f"dve_tokens{b}") for b in range(2)]
            for name in ("shared_hidden", "qkv_biased", "kv_masked", "masked", "x2_ready", "state_ready", "seen_ready", "base_ready"):
                dve.sem_inc(S[name], AHEAD)
            nc.vector.memset(empty[:], 0.0).then_inc(S["empty_set"], 1)
            nc.vector.memset(zeros[:], 0.0).then_inc(S["empty_set"], 1)
            nc.vector.memset(seen[:], 0.0).then_inc(S["empty_set"], 1)
            nc.vector.memset(state[:], 0.0).then_inc(S["empty_set"], 1)
            nc.vector.memset(cenT[:], 0.0).then_inc(S["empty_set"], 1)
            nc.vector.memset(kept[:], 0).then_inc(S["empty_set"], 1)
            dve.wait_ge(S["empty_set"], 6)
            nc.vector.memset(empty[:].bitcast(U32)[:, D + 1:D + 2], FAR).then_inc(S["empty_set"], 1)
            dve.wait_ge(S["first_x_in"], 16)
            norm_stats("h", 0, 0)
            dve.wait_ge(S["cen_in"], 16)
            nc.vector.tensor_tensor_reduce(cen_sq[:], cen[:], cen[:], 1.0, 0.0, ALU.mult, ALU.add,
                                           cen_n[:, 0:1]).then_inc(S["cen_square"], 1)
            norm_apply("h", 0, 0)
            dve.wait_ge(S["cen_root"], 1)
            nc.vector.tensor_scalar(cen_n[:, 2:3], cen_n[:, 1:2], 1e-12, None, ALU.max).then_inc(S["cen_inv0"], 1)
            dve.wait_ge(S["cen_inv0"], 1)
            nc.vector.reciprocal(cen_n[:, 3:4], cen_n[:, 2:3]).then_inc(S["cen_inv"], 1)
            dve.wait_ge(S["cen_inv"], 1)
            nc.vector.tensor_scalar(cen_sq[:], cen[:], cen_n[:, 3:4], None, ALU.mult).then_inc(S["cen_scaled"], 1)
            dve.wait_ge(S["cen_turned"], 1)
            nc.vector.tensor_copy(cenT[:, 0:NG + E], bank[2][:, 0:NG + E]).then_inc(S["cenT_ready"], 1)
            norm_lengths("h", 0)
            dve.wait_ge(S["x_in"], 16)
            norm_stats("i", 0, 1)
            dve.wait_ge(S["consts_in"], 32)
            dve.wait_ge(S["small_in"], 16 * 5)
            dve.wait_ge(S["norm_inv_h"], 1)
            for g in range(GROUPS):
                route_experts("i", g, g)
                if g == 0:
                    norm_apply("i", 0, 1, 0)
                    norm_lengths("i", 0)
                route_counts(g)
                route_slots("i", g, g, g % 2)
                if g + 2 < GROUPS:
                    norm_apply("i", 0, g + 2, (g + 1) * GT)
                if g == 0:
                    dve.wait_ge(S["norm_inv_i"], 1)
                shared_hidden("i", g, 0)
                shared_hidden("i", g, 1)
                shared_out("i", g, g)
            for b in range(2):
                nc.vector.memset(vp[b][:], 0.0).then_inc(S["empty_set"], 1)
            experts(0)
            dve.wait_ge(S["seen_ready"], (GT + 1) * GROUPS + AHEAD)
            nc.vector.memset(seen[:, 0, :], 0.0).then_inc(S["empty_set"], 1)
            dve.wait_ge(S["empty_set"], 10)
            combine(0, 0)
            dve.wait_ge(S["x1_ready"], 1)
            norm_stats("a", 0, 0)
            apply_a(0)
            bias_rope(0, 0)
            attention(0, -1, False, False)
            combine(0, 1)
            for j in range(GT):
                attention(0, j, False, True)
            with dve.Fori(1, GROUPS - 1) as g:
                for j in range(GT):
                    attention(g, j, True, True)
            for j in range(GT):
                attention(GROUPS - 1, j, True, False)
            attention(GROUPS - 1, GT, False, False)
            dve.wait_ge(S["x2_ready"], TILES + AHEAD)
            norm_stats("f", GROUPS - 1, GROUPS - 1)
            apply_f(2 * GROUPS - 1, GROUPS - 1)
            feed_forward("f", 2 * GROUPS - 1, GROUPS - 1, 1)
            experts(1)
            for g in range(GROUPS):
                combine(1, g)

        @block.scalar
        def _(act):
            def roots(kind, n):
                act.wait_ge(S[f"sq_ready_{kind}"], n + 1)
                nc.scalar.activation(rs[kind][:], sq[kind][:], ACT.Sqrt).then_inc(S[f"roots_{kind}"], 1)

            def turn_f(q):
                act.wait_ge(S["xf_turned_f"], q - GROUPS + 1 + AHEAD)
                act.wait_ge(S["gates_up"], HC * q + AHEAD)
                nc.scalar.activation(xfT["f"][:], bank[7][:], ACT.Copy).then_inc(S["xfT_ready_f"], 1)

            def turn_first(g):
                act.wait_ge(S["xf_turned_i"], g + 1)
                nc.scalar.activation(turned("i", g), bank[1][:], ACT.Copy).then_inc(S["xfT_ready_i"], 1)

            def turn_a(g):
                act.wait_ge(S["xf_turned_a"], g + 1 + AHEAD)
                act.wait_ge(S["qkv_out"], GT * g + AHEAD)
                nc.scalar.activation(xfT["a"][:], bank[0][:], ACT.Copy).then_inc(S["xfT_ready_a"], 1)

            def shared_gate(kind, q, c):
                act.wait_ge(S["gates_up"], HC * q + c + 1 + AHEAD)
                act.wait_ge(S["shared_hidden"], HC * q + AHEAD)
                nc.scalar.activation(gs[:, c, :], gates_of(kind, c)[:], ACT.Silu).then_inc(S["shared_gate"], 1)

            def fill_rows(kind, q, g, b):
                act.wait_ge(S["delta"], q + 1)
                nc.scalar.activation(th[:], dlt[:], ACT.Tanh, scale=0.5).then_inc(S["tanh_ready"], 1)
                if not (kind == "f" and b):
                    act.wait_ge(S["rows_free"], sent_before(kind, q))
                for j in range(GT):
                    i = nc.scalar.activation(rows_of(b)[:, j, :, 0:D], bc(normed(kind, g)[:, j, :], 1, K), ACT.Copy)
                i.then_inc(S["rows_x"], 1)

            def spread_values(g, j):
                act.wait_ge(S["qkv_biased"], GT * g + j + 1 + AHEAD)
                b = j % 2
                nc.scalar.activation(vp[b][:].rearrange("p (h x) -> p h x", h=HEADS)[:, :, 0:DH],
                                     qkv[b][:, 2 * D:].rearrange("p (h e) -> p h e", h=HEADS),
                                     ACT.Copy).then_inc(S["vp_ready"], 1)

            def attention(g, j, behind, ahead):
                q = g + (GROUPS - 1)
                t = GT * g + j
                if is_tile(g, j + 1):
                    act.wait_ge(S["qk_turned"], t + 2)
                    for h in range(HB):
                        i = nc.scalar.activation(qx[:, h, :], bank[2][:, 0:P], ACT.Copy, scale=head_mask[:, h:h + 1])
                    i.then_inc(S["qx_ready"], 1)
                    nc.scalar.activation(qkT[(j + 1) % 2][:], bank[2][:, 0:2 * P], ACT.Copy).then_inc(S["qkT_ready"], 1)
                    spread_values(g, j + 1)
                if j == 1:
                    if ahead:
                        turn_a(g + 1)
                    if behind:
                        turn_f(q)
                if j in (2, 3) and behind:
                    shared_gate("f", q, j - 2)
                if is_tile(g, j):
                    act.wait_ge(S["oT_out"], t + 1)
                    nc.scalar.activation(oT[:], bank[3][:, 0:P], ACT.Copy).then_inc(S["oT_ready"], 1)
                if j == 0:
                    if ahead:
                        roots("a", g + 1)
                    if behind:
                        roots("f", q - GROUPS)
                if j == 2 and behind:
                    fill_rows("f", q, g - 1, 0)

            def turn_x(f, i, d, sizes):
                e = expert(f, i, d)
                act.wait_ge(S["x_turned"], e + 1)
                act.wait_ge(S["e_up_out"], e - 1 if d else E * f)
                nc.scalar.activation(xbT[d % 2][:, 0:sum(sizes)], bank[0][:, 0:sum(sizes)], ACT.Copy).then_inc(S["xT_ready"], 1)

            def gate(f, i, d, width):
                e = expert(f, i, d)
                act.wait_ge(S["e_gate_out"], e + 1)
                act.wait_ge(S["e_hidden"], e)
                for c in range(HC):
                    a = nc.scalar.activation(eg[:, c, 0:width], bank[1 + c][:, 0:width], ACT.Silu)
                a.then_inc(S["e_gate_act"], 1)

            def scale(f, i, d, sizes):
                e = expert(f, i, d)
                act.wait_ge(S["e_down"], e + 1)
                act.wait_ge(S["results_free"], e + AHEAD)
                for t, m in enumerate(sizes):
                    a = nc.scalar.activation(eo[d % RB][0:m, t, :], bank[5 + d % 2][0:m, t * D:(t + 1) * D], ACT.Copy,
                                             scale=xb[d % XB][0:m, t, D:D + 1])
                a.then_inc(S["e_scaled"], 1)

            def experts(f):
                act.wait_ge(S["kept_ready"], f + 1)
                act.reg_load(tokens, kept[0:1, f, KEPT0:KEPT0 + XB + 2])
                with act.If_lt(tokens[0], P + 1):
                    turn_x(f, 0, 0, SIZES[:1])
                with act.Else():
                    with act.If_lt(tokens[0], 2 * P + 1):
                        turn_x(f, 0, 0, SIZES[:2])
                    with act.Else():
                        turn_x(f, 0, 0, SIZES)
                with act.If_lt(tokens[1], P + 1):
                    turn_x(f, 0, 1, SIZES[:1])
                with act.Else():
                    with act.If_lt(tokens[1], 2 * P + 1):
                        turn_x(f, 0, 1, SIZES[:2])
                    with act.Else():
                        turn_x(f, 0, 1, SIZES)
                with act.If_lt(tokens[0], P + 1):
                    gate(f, 0, 0, P)
                with act.Else():
                    with act.If_lt(tokens[0], 2 * P + 1):
                        gate(f, 0, 0, 2 * P)
                    with act.Else():
                        gate(f, 0, 0, CAP)

                def step(i, d):
                    if not (isinstance(i, int) and XB * i + d + 1 >= E):
                        with act.If_lt(tokens[d + 1], P + 1):
                            turn_x(f, i, d + 1, SIZES[:1])
                        with act.Else():
                            with act.If_lt(tokens[d + 1], 2 * P + 1):
                                turn_x(f, i, d + 1, SIZES[:2])
                            with act.Else():
                                turn_x(f, i, d + 1, SIZES)
                    with act.If_lt(tokens[d], P + 1):
                        gate(f, i, d, P)
                    with act.Else():
                        with act.If_lt(tokens[d], 2 * P + 1):
                            gate(f, i, d, 2 * P)
                        with act.Else():
                            gate(f, i, d, CAP)
                    with act.If_lt(tokens[d - 1], P + 1):
                        scale(f, i, d - 1, SIZES[:1])
                    with act.Else():
                        with act.If_lt(tokens[d - 1], 2 * P + 1):
                            scale(f, i, d - 1, SIZES[:2])
                        with act.Else():
                            scale(f, i, d - 1, SIZES)

                with act.Fori(0, E // XB - 1) as i:
                    act.reg_load(tokens, kept[0:1, f, bass.ds(XB * i + KEPT0, XB + 2)])
                    for d in range(1, XB + 1):
                        step(i, d)
                act.reg_load(tokens, kept[0:1, f, KEPT0 + E - XB:KEPT0 + E + 2])
                for d in range(1, XB):
                    step(E // XB - 1, d)
                with act.If_lt(tokens[XB - 1], P + 1):
                    scale(f, E // XB - 1, XB - 1, SIZES[:1])
                with act.Else():
                    with act.If_lt(tokens[XB - 1], 2 * P + 1):
                        scale(f, E // XB - 1, XB - 1, SIZES[:2])
                    with act.Else():
                        scale(f, E // XB - 1, XB - 1, SIZES)

            tokens = [act.alloc_register(f"act_tokens{d}") for d in range(XB + 2)]
            for name in ("xfT_ready_a", "xfT_ready_f", "qkT_ready", "e_scaled", "rows_x", "oT_ready"):
                act.sem_inc(S[name], AHEAD)
            roots("h", 0)
            act.wait_ge(S["cen_square"], 1)
            nc.scalar.activation(cen_n[:, 1:2], cen_n[:, 0:1], ACT.Sqrt).then_inc(S["cen_root"], 1)
            turn_first(0)
            roots("i", 0)
            for g in range(GROUPS):
                shared_gate("i", g, 0)
                shared_gate("i", g, 1)
                fill_rows("i", g, g, g % 2)
                if g == 0:
                    turn_first(1)
                if g + 2 < GROUPS:
                    turn_first(g + 2)
            experts(0)
            roots("a", 0)
            turn_a(0)
            attention(0, -1, False, False)
            for j in range(GT):
                attention(0, j, False, True)
            with act.Fori(1, GROUPS - 1) as g:
                for j in range(GT):
                    attention(g, j, True, True)
            for j in range(GT):
                attention(GROUPS - 1, j, True, False)
            last = 2 * GROUPS - 1
            roots("f", GROUPS - 1)
            turn_f(last)
            shared_gate("f", last, 0)
            fill_rows("f", last, GROUPS - 1, 1)
            shared_gate("f", last, 1)
            experts(1)

        @block.tensor
        def _(pe):
            def turn(kind, n):
                to = {"a": bank[0], "f": bank[7], "i": bank[1]}[kind]
                if kind == "f":
                    pe.wait_ge(S["base_ready"], n + GROUPS + AHEAD)
                for j in range(GT):
                    pe.wait_ge(S[f"xf_ready_{kind}"], GT * n + j + 1)
                    i = nc.tensor.transpose(to[:, j * P:(j + 1) * P], normed(kind, n)[:, j, :], ident)
                i.then_inc(S[f"xf_turned_{kind}"], 1)

            def router(kind, q, g):
                if kind == "f":
                    pe.wait_ge(S["xfT_ready_f"], q - GROUPS + 1 + AHEAD)
                for j in range(GT):
                    i = nc.tensor.matmul(bank[6][:, j * P:(j + 1) * P], turned(kind, g)[:, j * P:(j + 1) * P], cenT[:],
                                         start=True, stop=True)
                i.then_inc(S["router_out"], 1)

            def gate_up_shared(kind, q, g, c):
                if c and kind == "f":
                    pe.wait_ge(S["shared_gate"], HC * q + c)
                    pe.wait_ge(S["shared_hidden"], HC * q + c + AHEAD)
                xT = turned(kind, g)
                nc.tensor.matmul(gates_of(kind, c)[:], w_sgu[:, c * P:(c + 1) * P], xT, start=True, stop=True)
                nc.tensor.matmul(ups_of(kind, c)[:], w_sgu[:, H + c * P:H + (c + 1) * P], xT, start=True,
                                 stop=True).then_inc(S["gates_up"], 1)

            def prefix(q):
                pe.wait_ge(S["seen_ready"], (GT + 1) * q + GT + AHEAD)
                nc.tensor.matmul(bank[6][:, 0:GT * E], strict, cnt[:].rearrange("p j e -> p (j e)"), start=True, stop=False)
                nc.tensor.matmul(bank[6][:, 0:GT * E], ones, seen[:, 0:GT, :].rearrange("p j e -> p (j e)"),
                                 start=False, stop=True).then_inc(S["prefix_out"], 1)

            def totals(f):
                pe.wait_ge(S["seen_ready"], (GT + 1) * GROUPS * (f + 1) + AHEAD)
                nc.tensor.matmul(bank[6][:, 0:E], ones, seen[:, 0, :], start=True, stop=True).then_inc(S["totals_out"], 1)

            def down_shared(kind, q):
                if kind == "i":
                    pe.wait_ge(S["base_ready"], q + AHEAD)
                pe.wait_ge(S["shared_hidden"], HC * (q + 1) + AHEAD)
                for j in range(GT):
                    for c in range(HC):
                        i = nc.tensor.matmul(out_of(kind)[:, j * D:(j + 1) * D], hs[:, c, j * P:(j + 1) * P],
                                             w_sd[:, c * D:(c + 1) * D], start=(c == 0), stop=(c == HC - 1))
                i.then_inc(S["shared_out"], 1)

            def turn_x(f, i, d, sizes):
                e = expert(f, i, d)
                pe.wait_ge(s_xb[d % XB], (i + (E // XB * f + d // XB + 1)) * 32)
                pe.wait_ge(S["xT_ready"], e)
                for t, m in enumerate(sizes):
                    a = nc.tensor.transpose(bank[0][:, t * P:t * P + m], xb[d % XB][0:m, t, 0:D], ident[0:m, 0:m])
                a.then_inc(S["x_turned"], 1)

            def gate_up(f, i, d, sizes):
                width = sum(sizes)
                e = expert(f, i, d)
                w = w_e[d % XB]
                pe.wait_ge(s_w[d % XB], (i + (E // XB * f + d // XB + 1)) * 16)
                pe.wait_ge(S["xT_ready"], e + 1)
                pe.wait_ge(S["e_gate_act"], e)
                for c in range(2 * HC):
                    if c == HC:
                        pe.wait_ge(S["e_hidden"], e)
                    a = nc.tensor.matmul(bank[1 + c][:, 0:width], w[:, c * P:(c + 1) * P], xbT[d % 2][:, 0:width], start=True, stop=True)
                    if c == HC - 1:
                        a.then_inc(S["e_gate_out"], 1)
                a.then_inc(S["e_up_out"], 1)

            def down(f, i, d, sizes):
                e = expert(f, i, d)
                pe.wait_ge(S["e_hidden"], e + 1)
                pe.wait_ge(S["e_scaled"], e + AHEAD)
                for t, m in enumerate(sizes):
                    for c in range(HC):
                        a = nc.tensor.matmul(bank[5 + d % 2][0:m, t * D:(t + 1) * D], eh[d % 2][:, c, t * P:t * P + m],
                                             w_e[d % XB][:, 2 * H + c * D:2 * H + (c + 1) * D],
                                             start=(c == 0), stop=(c == HC - 1))
                a.then_inc(S["e_down"], 1)

            def experts(f):
                pe.wait_ge(S["kept_ready"], f + 1)
                pe.reg_load(tokens, kept[0:1, f, KEPT0:KEPT0 + XB + 2])
                with pe.If_lt(tokens[0], P + 1):
                    turn_x(f, 0, 0, SIZES[:1])
                with pe.Else():
                    with pe.If_lt(tokens[0], 2 * P + 1):
                        turn_x(f, 0, 0, SIZES[:2])
                    with pe.Else():
                        turn_x(f, 0, 0, SIZES)
                with pe.If_lt(tokens[1], P + 1):
                    turn_x(f, 0, 1, SIZES[:1])
                with pe.Else():
                    with pe.If_lt(tokens[1], 2 * P + 1):
                        turn_x(f, 0, 1, SIZES[:2])
                    with pe.Else():
                        turn_x(f, 0, 1, SIZES)
                with pe.If_lt(tokens[0], P + 1):
                    gate_up(f, 0, 0, SIZES[:1])
                with pe.Else():
                    with pe.If_lt(tokens[0], 2 * P + 1):
                        gate_up(f, 0, 0, SIZES[:2])
                    with pe.Else():
                        gate_up(f, 0, 0, SIZES)

                def step(i, d):
                    if not (isinstance(i, int) and XB * i + d + 1 >= E):
                        with pe.If_lt(tokens[d + 1], P + 1):
                            turn_x(f, i, d + 1, SIZES[:1])
                        with pe.Else():
                            with pe.If_lt(tokens[d + 1], 2 * P + 1):
                                turn_x(f, i, d + 1, SIZES[:2])
                            with pe.Else():
                                turn_x(f, i, d + 1, SIZES)
                    with pe.If_lt(tokens[d], P + 1):
                        gate_up(f, i, d, SIZES[:1])
                    with pe.Else():
                        with pe.If_lt(tokens[d], 2 * P + 1):
                            gate_up(f, i, d, SIZES[:2])
                        with pe.Else():
                            gate_up(f, i, d, SIZES)
                    with pe.If_lt(tokens[d - 1], P + 1):
                        down(f, i, d - 1, SIZES[:1])
                    with pe.Else():
                        with pe.If_lt(tokens[d - 1], 2 * P + 1):
                            down(f, i, d - 1, SIZES[:2])
                        with pe.Else():
                            down(f, i, d - 1, SIZES)

                with pe.Fori(0, E // XB - 1) as i:
                    pe.reg_load(tokens, kept[0:1, f, bass.ds(XB * i + KEPT0, XB + 2)])
                    for d in range(1, XB + 1):
                        step(i, d)
                pe.reg_load(tokens, kept[0:1, f, KEPT0 + E - XB:KEPT0 + E + 2])
                for d in range(1, XB):
                    step(E // XB - 1, d)
                with pe.If_lt(tokens[XB - 1], P + 1):
                    down(f, E // XB - 1, XB - 1, SIZES[:1])
                with pe.Else():
                    with pe.If_lt(tokens[XB - 1], 2 * P + 1):
                        down(f, E // XB - 1, XB - 1, SIZES[:2])
                    with pe.Else():
                        down(f, E // XB - 1, XB - 1, SIZES)

            def project(g, j):
                pe.wait_ge(S["xfT_ready_a"], g + (j // GT + 1 + AHEAD))
                pe.wait_ge(S["qkv_biased"], GT * g + j + AHEAD)
                nc.tensor.matmul(bank[1][:, 0:3 * D], xfT["a"][:, j % GT * P:(j % GT + 1) * P], w_qkv[:], start=True,
                                 stop=True).then_inc(S["qkv_out"], 1)

            def scores(g, j, h):
                pe.wait_ge(S["qx_ready"], GT * g + j + 1)
                pe.wait_ge(S["masked"], 4 * GT * g + (4 * j + h - 1 + AHEAD))
                nc.tensor.matmul(bank[4 + h % 2][:], qkT[j % 2][32 * h:32 * h + 32, P:2 * P],
                                 qx[32 * h:32 * h + 32, :, :].rearrange("p h t -> p (h t)"), start=True,
                                 stop=True).then_inc(S["score_out"], 1)

            def weigh_values(g, j, h):
                pe.wait_ge(S["masked"], 4 * GT * g + (4 * j + h + 1 + AHEAD))
                for n in range(HB * h, HB * (h + 1)):
                    i = nc.tensor.matmul(bank[3][:, 0:P], vp[j % 2][:, n * D:(n + 1) * D],
                                         pr[j % 2][:, h, n % HB * P:(n % HB + 1) * P],
                                         start=False, stop=(n == HEADS - 1))
                if h == HEADS // HB - 1:
                    i.then_inc(S["oT_out"], 1)

            def attention(g, j, behind, ahead):
                q = g + (GROUPS - 1)
                t = GT * g + j
                now, after = is_tile(g, j), is_tile(g, j + 1)
                if after:
                    b = (j + 1) % 2
                    pe.wait_ge(S["rope_ready"], t + 2)
                    pe.wait_ge(S["kv_masked"], t + 1 + AHEAD)
                    nc.tensor.transpose(bank[2][:, 0:P], qk[b][:, 0:D], ident)
                    nc.tensor.transpose(bank[2][:, P:2 * P], qk[b][:, D:], ident).then_inc(S["qk_turned"], 1)
                if now:
                    pe.wait_ge(S["oT_ready"], t + AHEAD)
                    pe.wait_ge(S["state_ready"], t + AHEAD)
                    nc.tensor.matmul(bank[3][:, 0:P], state[:], qkT[j % 2][:, 0:P], start=True,
                                     stop=False).then_inc(S["state_read"], 1)
                    pe.wait_ge(S["vp_ready"], t + 1)
                    weigh_values(g, j, 0)
                if is_tile(g, j + 2):
                    project(g, j + 2)
                if now:
                    weigh_values(g, j, 1)
                if after:
                    pe.wait_ge(S["qkT_ready"], t + 2 + AHEAD)
                    nc.tensor.matmul(bank[2][:, 0:D], qk[b][:, D:], qkv[b][:, 2 * D:], start=True,
                                     stop=True).then_inc(S["kv_out"], 1)
                if j == 1:
                    if ahead:
                        turn("a", g + 1)
                    if behind:
                        turn("f", q - GROUPS)
                if is_tile(g, j - 1):
                    if j % GT == 0:
                        pe.wait_ge(S["pos_part"], q + j // GT)
                    if j == 2 and behind:
                        pe.wait_ge(S["scores_n"], q + 1)
                    pe.wait_ge(S["oT_ready"], t + AHEAD)
                    pe.wait_ge(S["x2_ready"], t - 1 + AHEAD)
                    nc.tensor.transpose(bank[6][:, 0:D], oT[:], ident).then_inc(S["attn_out"], 1)
                if after:
                    scores(g, j + 1, 0)
                    scores(g, j + 1, 1)
                if now:
                    weigh_values(g, j, 2)
                if behind and j in (1, 3):
                    pe.wait_ge(S["x2_ready"], t + AHEAD)
                if behind and j == 1:
                    router("f", q, g - 1)
                if behind and j == 3:
                    prefix(q)
                if behind and j >= 2:
                    gate_up_shared("f", q, g - 1, j - 2)
                if after:
                    scores(g, j + 1, 2)
                if now:
                    weigh_values(g, j, 3)
                if after:
                    scores(g, j + 1, 3)
                if behind and j == 3:
                    down_shared("f", q)

            tokens = [pe.alloc_register(f"pe_tokens{d}") for d in range(XB + 2)]
            for name in ("xf_turned_a", "xf_turned_f", "gates_up", "qkv_out"):
                pe.sem_inc(S[name], AHEAD)
            pe.wait_ge(S["consts_in"], 32)
            pe.wait_ge(S["empty_set"], 7)
            turn("i", 0)
            pe.wait_ge(S["cen_scaled"], 1)
            nc.tensor.transpose(bank[2][:, 0:NG + E], cen_sq[:], ident[0:NG + E, 0:NG + E]).then_inc(S["cen_turned"], 1)
            pe.wait_ge(S["cenT_ready"], 1)
            pe.wait_ge(S["xfT_ready_i"], 1)
            router("i", 0, 0)
            pe.wait_ge(S["small_in"], 16 * 5)
            for g in range(GROUPS):
                gate_up_shared("i", g, g, 0)
                gate_up_shared("i", g, g, 1)
                if g == 0:
                    turn("i", 1)
                prefix(g)
                if g + 1 < GROUPS:
                    pe.wait_ge(S["xfT_ready_i"], g + 2)
                    pe.wait_ge(S["pos_part"], g + 1)
                    router("i", g + 1, g + 1)
                down_shared("i", g)
                if g + 2 < GROUPS:
                    turn("i", g + 2)
            totals(0)
            pe.wait_ge(S["base_ready"], GROUPS + AHEAD)
            experts(0)
            pe.wait_ge(S["e_scaled"], E + AHEAD)
            turn("a", 0)
            project(0, 0)
            attention(0, -1, False, False)
            for j in range(GT):
                attention(0, j, False, True)
            with pe.Fori(1, GROUPS - 1) as g:
                for j in range(GT):
                    attention(g, j, True, True)
            for j in range(GT):
                attention(GROUPS - 1, j, True, False)
            attention(GROUPS - 1, GT, False, False)
            last = 2 * GROUPS - 1
            turn("f", GROUPS - 1)
            router("f", last, GROUPS - 1)
            gate_up_shared("f", last, GROUPS - 1, 0)
            prefix(last)
            gate_up_shared("f", last, GROUPS - 1, 1)
            down_shared("f", last)
            totals(1)
            pe.wait_ge(S["base_ready"], 2 * GROUPS + AHEAD)
            experts(1)

        @block.gpsimd
        def _(pool):
            def dispatch(f, q, b):
                rows = rows_of(b)
                pool.wait_ge(S["rows_gate"], q + 1)
                pool.wait_ge(S["rows_x"], q + 1 + AHEAD)
                pool.sem_inc(passed["pool"], 1)
                for j in range(GT):
                    for k in range(K):
                        pool.indirect_dma_start(
                            slots[f], bass.IndirectOffsetOnAxis(ap=slot[b][:, j * K + k:j * K + k + 1], axis=0),
                            rows[:, j, k, :], None, bounds_check=last_slot, oob_is_err=False).then_inc(s_rows[b], 16)

            def send(f, d, tiles, signal):
                for t in tiles:
                    m = SIZES[t]
                    pool.indirect_dma_start(
                        routed[f], bass.IndirectOffsetOnAxis(ap=xb[d].bitcast(U32)[0:m, t, D + 1:D + 2], axis=0),
                        eo[d % RB][0:m, t, :], None, bounds_check=last_place, oob_is_err=False).then_inc(signal, 16)

            def results(f, i, d):
                pool.wait_ge(S["e_scaled"], expert(f, i, d) + 1 + AHEAD)
                pool.sem_inc(passed["pool"], 1)
                send(f, d, [0], s_first[d % RB])
                for t in range(1, ST):
                    with pool.If_lt(whole_tiles[t - 1], tokens[d + 2]):
                        send(f, d, [t], s_others[d % RB])
                        pool.reg_add(others[d % RB], others[d % RB], 16)
                if not (isinstance(i, int) and d < 2):
                    arrived(f, i, d - 2)

            def arrived(f, i, d):
                pool.wait_ge(s_first[d % RB], i * (XB // RB * 16) + ((E * f + d) // RB + 1) * 16)
                pool.sem_inc(passed["pool"], 1)
                with pool.If_lt(whole_tiles[0], tokens[d + 2]):
                    pool.wait_ge(s_others[d % RB], others[d % RB])
                    pool.sem_inc(passed["pool"], 1)
                pool.sem_inc(S["results_free"], 1)

            tokens = [pool.alloc_register(f"pool_tokens{d}") for d in range(XB + 2)]
            others = [pool.alloc_register(f"pool_others{b}") for b in range(RB)]
            whole_tiles = [pool.alloc_register(f"whole_tiles{t}") for t in range(ST - 1)]
            for t in range(ST - 1):
                pool.reg_mov(whole_tiles[t], (t + 1) * P)
            for b in range(RB):
                pool.reg_mov(others[b], 0)
            pool.sem_inc(S["rows_free"], 2 * AHEAD)
            pool.sem_inc(S["results_free"], RB * AHEAD)
            last_slot = pool.to_reg(SLOTS - 1)
            last_place = pool.to_reg(TOKENS * K - 1)
            pool.wait_ge(S["empty_sent0"], 16 * FILLS)
            for g in range(GROUPS):
                dispatch(0, g, g % 2)
                if g:
                    pool.wait_ge(s_rows[(g - 1) % 2], ((g - 1) // 2 + 1) * (16 * GT * K))
                    pool.sem_inc(S["rows_free"], 1)
            pool.wait_ge(s_rows[1], GROUPS // 2 * (16 * GT * K))
            pool.sem_inc(S["rows_free"], 1)
            pool.wait_ge(S["zeros_sent0"], 16 * FILLS)
            pool.wait_ge(S["kept_ready"], 1)
            pool.reg_load(tokens, kept[0:1, 0, KEPT0 - 2:KEPT0 + XB])
            for d in range(XB):
                results(0, 0, d)
            with pool.Fori(1, E // XB) as i:
                pool.reg_load(tokens, kept[0:1, 0, bass.ds(XB * i + (KEPT0 - 2), XB + 2)])
                for d in range(XB):
                    results(0, i, d)
            arrived(0, E // XB - 1, XB - 2)
            arrived(0, E // XB - 1, XB - 1)
            pool.wait_ge(S["empty_sent1"], 16 * FILLS)
            with pool.Fori(0, GROUPS - 1) as g:
                dispatch(1, GROUPS + g, 0)
                pool.wait_ge(s_rows[0], (g + (GROUPS // 2 + 1)) * (16 * GT * K))
                pool.sem_inc(S["rows_free"], 1)
            dispatch(1, 2 * GROUPS - 1, 1)
            pool.wait_ge(S["zeros_sent1"], 16 * FILLS)
            pool.wait_ge(S["kept_ready"], 2)
            pool.reg_load(tokens, kept[0:1, 1, KEPT0 - 2:KEPT0 + XB])
            for d in range(XB):
                results(1, 0, d)
            with pool.Fori(1, E // XB) as i:
                pool.reg_load(tokens, kept[0:1, 1, bass.ds(XB * i + (KEPT0 - 2), XB + 2)])
                for d in range(XB):
                    results(1, i, d)
            arrived(1, E // XB - 1, XB - 2)
            arrived(1, E // XB - 1, XB - 1)

        @block.sync
        def _(sp):
            def load_weights(b, e):
                sp.dma_start(w_e[b][:], ew[bass.ds(e, 1), :, :].rearrange("e p n -> (e p) n")).then_inc(s_w[b], 16)

            def load_slots(f, b, e):
                src = slots[f]
                sp.dma_start(xb[b][:, 0:FULL, :], src[bass.ds(e * CAP, FULL * P), :].rearrange("(t p) r -> p t r", p=P)
                             ).then_inc(s_xb[b], 16)
                sp.dma_start(xb[b][0:REST, FULL, :], src[bass.ds(e * CAP + FULL * P, REST), :]).then_inc(s_xb[b], 16)

            def fill_slots(f, c):
                a = slots[f].rearrange("(p n) r -> p n r", n=SLOTS // (P * FILLS))
                sp.dma_start(a[bass.ds(c * P, P), :, :], bc(empty[:], 1, SLOTS // (P * FILLS))).then_inc(S[f"empty_sent{f}"], 16)

            def fill_routed(f, c):
                z = routed[f].rearrange("(p n) d -> p n d", n=TOKENS * K // (P * FILLS))
                sp.dma_start(z[bass.ds(c * P, P), :, :], bc(zeros[:], 1, TOKENS * K // (P * FILLS))).then_inc(S[f"zeros_sent{f}"], 16)

            sp.dma_start(xres[:, 0:GW].rearrange("p (t d) -> p t d", t=GT), x_t[:, 0:GT, :]).then_inc(S["first_x_in"], 16)
            sp.dma_start(cen[:], cents).then_inc(S["cen_in"], 16)
            sp.dma_start(cst[:], consts).then_inc(S["consts_in"], 16)
            sp.dma_start(plc[:], places).then_inc(S["consts_in"], 16)
            sp.dma_start(xres[:, GW:].rearrange("p (t d) -> p t d", t=TILES - GT), x_t[:, GT:, :]).then_inc(S["x_in"], 16)
            sp.dma_start(w_sgu[:], sgu).then_inc(S["small_in"], 16)
            sp.dma_start(w_sd[:].rearrange("p (c d) -> p c d", c=HC), sd.rearrange("(c p) d -> p c d", p=P)).then_inc(S["small_in"], 16)
            sp.dma_start(w_qkv[:], wqkv).then_inc(S["small_in"], 16)
            sp.dma_start(b_qkv[:], bqkv.to_broadcast([P, 3 * D])).then_inc(S["small_in"], 16)
            sp.dma_start(e_bias[:], ebias.to_broadcast([P, E])).then_inc(S["small_in"], 16)
            sp.wait_ge(S["empty_set"], 7)
            for c in range(FILLS):
                fill_slots(0, c)
            for f in range(2):
                if f == 0:
                    sp.wait_ge(S["slot_ready"], 2)
                    for c in range(FILLS):
                        fill_routed(0, c)
                for d in range(XB):
                    load_weights(d, d)
                sp.wait_ge(s_rows[0], 16 * K * GT * (GROUPS // 2 + (GROUPS - 1) * f))
                sp.wait_ge(s_rows[1], 16 * K * GT * (GROUPS // 2 + f))
                for d in range(XB):
                    load_slots(f, d, d)
                with sp.Fori(0, E // XB - 1) as i:
                    for d in range(XB):
                        sp.wait_ge(S["e_down"], expert(f, i, d) + 1)
                        sp.sem_inc(passed["sp"], 1)
                        load_weights(d, expert(0, i, d) + XB)
                        sp.wait_ge(S["results_free"], expert(f, i, d) + (1 + RB * AHEAD))
                        sp.sem_inc(passed["sp"], 1)
                        load_slots(f, d, expert(0, i, d) + XB)
                sp.wait_ge(S["results_free"], E * (f + 1) + RB * AHEAD)
                for g in range(GROUPS):
                    sp.dma_start(yk[:, g * GW * K:(g + 1) * GW * K].rearrange("p (j x) -> p j x", j=GT),
                                 routed[f][g * GW * K:(g + 1) * GW * K, :].rearrange("(j p k) d -> p j (k d)", p=P, k=K)
                                 ).then_inc(s_yk[g], 16)
                if f == 0:
                    for c in range(FILLS):
                        fill_slots(1, c)
                    for c in range(FILLS):
                        fill_routed(1, c)
                if f:
                    with sp.Fori(0, GROUPS) as g:
                        sp.wait_ge(S["x1_ready"], g + (GROUPS + 1))
                        sp.sem_inc(passed["sp"], 1)
                        sp.dma_start(out_t[:, bass.ds(g * GT, GT), :], xres_of(g)).then_inc(S["out_sent"], 16)
            sp.wait_ge(S["out_sent"], 16 * GROUPS)


def kernel(L0_attn_x, L0_attn_W_qkv, L0_attn_b_qkv, L0_ffn_group_centroids, L0_ffn_expert_centroids, L0_ffn_bias,
           L0_ffn_wg, L0_ffn_wu, L0_ffn_wd, L0_ffn_sg, L0_ffn_su, L0_ffn_sd):
    import concourse.bacc as bacc
    from concourse.bass_utils import run_bass_kernel_spmd

    n = np.asarray
    consts, places = shape_constants()
    wd = n(L0_ffn_wd).reshape(E, HC, P, D).transpose(0, 2, 1, 3).reshape(E, P, HC * D)
    ins = {
        "x": n(L0_attn_x).reshape(TOKENS, D),
        "consts": consts,
        "places": places,
        "wqkv": n(L0_attn_W_qkv).T,
        "bqkv": n(L0_attn_b_qkv).reshape(1, 3 * D),
        "cents": np.concatenate([n(L0_ffn_group_centroids), n(L0_ffn_expert_centroids)], 0),
        "ebias": n(L0_ffn_bias).reshape(1, E),
        "ew": np.concatenate([n(L0_ffn_wg), n(L0_ffn_wu), wd], 2),
        "sgu": np.concatenate([n(L0_ffn_sg), n(L0_ffn_su)], 1),
        "sd": n(L0_ffn_sd),
    }
    ins = {k: np.ascontiguousarray(v) for k, v in ins.items()}
    nc = bacc.Bacc("TRN2", target_bir_lowering=False, num_devices=1)
    args = {k: nc.dram_tensor(k, v.shape, mybir.dt.from_np(v.dtype), kind="ExternalInput").ap() for k, v in ins.items()}
    args["out"] = nc.dram_tensor("out", (TOKENS, D), F32, kind="ExternalOutput").ap()
    macaron(nc, **args)
    r = run_bass_kernel_spmd(nc, [ins], core_ids=[0])
    return r.results[0]["out"].reshape(1, TOKENS, D)
```
